# Optimizing a Trainium2 kernel written in Bass

```python
import numpy as np
import jax
import jax.numpy as jnp

def _softmax(x, axis=-1):
    return jax.nn.softmax(x, axis=axis)

def _gelu(x):
    return jax.nn.gelu(x, approximate=True)

def _silu(x):
    return jax.nn.silu(x)

def _sigmoid(x):
    return jax.nn.sigmoid(x)

def _layernorm(x, axis=-1, eps=1e-05):
    m = jnp.mean(x, axis=axis, keepdims=True)
    v = jnp.var(x, axis=axis, keepdims=True)
    return (x - m) / jnp.sqrt(v + eps)

def _scatter_add(tgt, idx, src, axis=0):
    return tgt.at[idx].add(src)

def _segment_sum(src, seg, n):
    return jax.ops.segment_sum(src, seg, n)
kernel_name = 'mk_adaln_d1_jaxref_r2_265d9d'

def setup_inputs(seed: int=0):
    np.random.seed(seed)
    _w = jnp.asarray

    def _L0_attn_setup():
        import jax, jax.numpy as jnp
        import numpy as np
        D_MODEL = 512
        N_HEADS = 16
        HEAD_DIM = D_MODEL // N_HEADS
        WINDOW = 256
        PREFIX = 16
        B = 2
        S = 2048

        def _windowed_global_attention(q, k, v):
            Bb, H, S_, Dh = q.shape
            W, P = (WINDOW, PREFIX)
            C = S_ // W
            scale = 1.0 / np.sqrt(Dh).astype(np.float32)
            qc = q.reshape(Bb, H, C, W, Dh)
            kp = jnp.pad(k, ((0, 0), (0, 0), (W, 0), (0, 0)))
            vp = jnp.pad(v, ((0, 0), (0, 0), (W, 0), (0, 0)))
            tail_idx = jnp.arange(C)[:, None] * W + jnp.arange(2 * W)[None, :]
            kt = kp[:, :, tail_idx, :]
            vt = vp[:, :, tail_idx, :]
            kg = k[:, :, :P, :]
            vg = v[:, :, :P, :]
            sg = jnp.einsum('bhcqd,bhkd->bhcqk', qc, kg) * scale
            st = jnp.einsum('bhcqd,bhckd->bhcqk', qc, kt) * scale
            q_pos = jnp.arange(C)[:, None] * W + jnp.arange(W)[None, :]
            kt_pos = jnp.arange(C)[:, None] * W - W + jnp.arange(2 * W)[None, :]
            mg = jnp.arange(P)[None, None, :] <= q_pos[:, :, None]
            diff = q_pos[:, :, None] - kt_pos[:, None, :]
            mt = (diff >= 0) & (diff < W) & (kt_pos[:, None, :] >= P)
            neg = jnp.asarray(-1000000000.0, sg.dtype)
            scores = jnp.concatenate([jnp.where(mg[None, None], sg, neg), jnp.where(mt[None, None], st, neg)], axis=-1)
            attn = jax.nn.softmax(scores, axis=-1)
            vcat = jnp.concatenate([jnp.broadcast_to(vg[:, :, None], (Bb, H, C, P, Dh)), vt], axis=3)
            out = jnp.einsum('bhcqk,bhckd->bhcqd', attn, vcat)
            return out.reshape(Bb, H, S_, Dh)
        key = jax.random.key(seed)
        k1, k2, k3 = jax.random.split(key, 3)
        x = jax.random.normal(k1, (B, S, D_MODEL), dtype=jnp.float32)
        w_qkv = jax.random.normal(k2, (3 * D_MODEL, D_MODEL), dtype=jnp.float32) * 0.02
        w_out = jax.random.normal(k3, (D_MODEL, D_MODEL), dtype=jnp.float32) * 0.02
        return {'x': x, 'w_qkv': w_qkv, 'w_out': w_out}
    _L0_attn_in = _L0_attn_setup()

    def _L0_ffn_setup():
        import jax, jax.numpy as jnp
        import numpy as np
        D_MODEL = 512
        M = 64
        INNER = 16
        key = jax.random.key(seed)
        ks = jax.random.split(key, 9)

        def init(k, shape, fan_in):
            bound = 1.0 / np.sqrt(fan_in)
            return jax.random.uniform(k, shape, jnp.float32, -bound, bound)
        x = jax.random.normal(ks[0], (16, 2048, D_MODEL), dtype=jnp.float32)
        Win = init(ks[1], (D_MODEL, M), D_MODEL)
        bin_ = init(ks[2], (M,), D_MODEL)
        W1 = init(ks[3], (M, INNER), 1)
        b1 = init(ks[4], (M, INNER), 1)
        W2 = init(ks[5], (M, INNER), INNER)
        b2 = init(ks[6], (M,), INNER)
        Wout = init(ks[7], (M, D_MODEL), M)
        bout = init(ks[8], (D_MODEL,), M)
        return {'x': x, 'Win': Win, 'bin_': bin_, 'W1': W1, 'b1': b1, 'W2': W2, 'b2': b2, 'Wout': Wout, 'bout': bout}
    _L0_ffn_in = _L0_ffn_setup()
    _L0_c = _w((lambda *s: np.random.randn(*s).astype(np.float32) * 0.05)(8, 512))
    _L0_wmod = _w((lambda *s: np.random.randn(*s).astype(np.float32) * 0.05)(512, 6 * 512) * 512 ** (-0.5))
    _d = {'L0_attn_x': _L0_attn_in['x'], 'L0_attn_w_qkv': _L0_attn_in['w_qkv'], 'L0_attn_w_out': _L0_attn_in['w_out'], 'L0_ffn_Win': _L0_ffn_in['Win'], 'L0_ffn_bin_': _L0_ffn_in['bin_'], 'L0_ffn_W1': _L0_ffn_in['W1'], 'L0_ffn_b1': _L0_ffn_in['b1'], 'L0_ffn_W2': _L0_ffn_in['W2'], 'L0_ffn_b2': _L0_ffn_in['b2'], 'L0_ffn_Wout': _L0_ffn_in['Wout'], 'L0_ffn_bout': _L0_ffn_in['bout'], 'L0_c': _L0_c, 'L0_wmod': _L0_wmod}
    _x0 = _d['L0_attn_x']
    _d['L0_attn_x'] = jax.random.normal(jax.random.fold_in(jax.random.key(seed), 1), (8, 2048, 512), dtype=_x0.dtype)
    del _x0
    return _d

def reference(L0_attn_x, L0_attn_w_qkv, L0_attn_w_out, L0_ffn_Win, L0_ffn_bin_, L0_ffn_W1, L0_ffn_b1, L0_ffn_W2, L0_ffn_b2, L0_ffn_Wout, L0_ffn_bout, L0_c, L0_wmod):

    def _L0_attn_ref(x, w_qkv, w_out):
        import jax, jax.numpy as jnp
        import numpy as np
        D_MODEL = 512
        N_HEADS = 16
        HEAD_DIM = D_MODEL // N_HEADS
        WINDOW = 256
        PREFIX = 16
        B = 2
        S = 2048

        def _windowed_global_attention(q, k, v):
            Bb, H, S_, Dh = q.shape
            W, P = (WINDOW, PREFIX)
            C = S_ // W
            scale = 1.0 / np.sqrt(Dh).astype(np.float32)
            qc = q.reshape(Bb, H, C, W, Dh)
            kp = jnp.pad(k, ((0, 0), (0, 0), (W, 0), (0, 0)))
            vp = jnp.pad(v, ((0, 0), (0, 0), (W, 0), (0, 0)))
            tail_idx = jnp.arange(C)[:, None] * W + jnp.arange(2 * W)[None, :]
            kt = kp[:, :, tail_idx, :]
            vt = vp[:, :, tail_idx, :]
            kg = k[:, :, :P, :]
            vg = v[:, :, :P, :]
            sg = jnp.einsum('bhcqd,bhkd->bhcqk', qc, kg) * scale
            st = jnp.einsum('bhcqd,bhckd->bhcqk', qc, kt) * scale
            q_pos = jnp.arange(C)[:, None] * W + jnp.arange(W)[None, :]
            kt_pos = jnp.arange(C)[:, None] * W - W + jnp.arange(2 * W)[None, :]
            mg = jnp.arange(P)[None, None, :] <= q_pos[:, :, None]
            diff = q_pos[:, :, None] - kt_pos[:, None, :]
            mt = (diff >= 0) & (diff < W) & (kt_pos[:, None, :] >= P)
            neg = jnp.asarray(-1000000000.0, sg.dtype)
            scores = jnp.concatenate([jnp.where(mg[None, None], sg, neg), jnp.where(mt[None, None], st, neg)], axis=-1)
            attn = jax.nn.softmax(scores, axis=-1)
            vcat = jnp.concatenate([jnp.broadcast_to(vg[:, :, None], (Bb, H, C, P, Dh)), vt], axis=3)
            out = jnp.einsum('bhcqk,bhckd->bhcqd', attn, vcat)
            return out.reshape(Bb, H, S_, Dh)
        Bb, S_, Dm = x.shape
        qkv = x @ w_qkv.T
        q, k, v = jnp.split(qkv, 3, axis=-1)

        def heads(t):
            return t.reshape(Bb, S_, N_HEADS, HEAD_DIM).transpose(0, 2, 1, 3)
        q, k, v = (heads(q), heads(k), heads(v))
        o = _windowed_global_attention(q, k, v)
        o = o.transpose(0, 2, 1, 3).reshape(Bb, S_, Dm)
        return o @ w_out.T

    def _L0_ffn_ref(x, Win, bin_, W1, b1, W2, b2, Wout, bout):
        import jax, jax.numpy as jnp
        import numpy as np
        D_MODEL = 512
        M = 64
        INNER = 16
        s = jnp.einsum('btd,dm->btm', x, Win) + bin_
        h = jax.nn.relu(s[..., None] * W1 + b1)
        g = jnp.einsum('btmh,mh->btm', h, W2) + b2
        out = jnp.einsum('btm,md->btd', g, Wout) + bout
        return out
    x = L0_attn_x
    mod = (_silu(L0_c) @ L0_wmod).reshape(L0_c.shape[0], 6, 1, -1)
    sa, ca, ga, sb, cb, gb = (mod[:, 0], mod[:, 1], mod[:, 2], mod[:, 3], mod[:, 4], mod[:, 5])
    ga = (2 * (ga >= 0) - 1) * jnp.maximum(jnp.abs(ga), 0.25)
    gb = (2 * (gb >= 0) - 1) * jnp.maximum(jnp.abs(gb), 0.25)
    h = _layernorm(x, axis=-1) * (1 + ca) + sa
    x = x + ga * _L0_attn_ref(h, L0_attn_w_qkv, L0_attn_w_out)
    h = _layernorm(x, axis=-1) * (1 + cb) + sb
    x = x + gb * _L0_ffn_ref(h, L0_ffn_Win, L0_ffn_bin_, L0_ffn_W1, L0_ffn_b1, L0_ffn_W2, L0_ffn_b2, L0_ffn_Wout, L0_ffn_bout)
    return x

_drawn_inputs = setup_inputs


def setup_inputs(seed=0):
    import zlib

    import numpy as np

    out = dict(_drawn_inputs(seed))
    spreads = {}
    factors = {'L0_attn_w_qkv': 8.0,
     'L0_attn_w_out': 8.0,
     'L0_ffn_Win': 3.399,
     'L0_ffn_bin_': 64.0,
     'L0_ffn_W1': 3.33,
     'L0_ffn_bout': 9.96,
     'L0_ffn_b1': 5.38,
     'L0_ffn_b2': 7.31}
    for name, (base, spread) in spreads.items():
        noise = np.random.default_rng([zlib.crc32(name.encode()), seed]).standard_normal(out[name].shape)
        drawn = base * np.exp(spread * noise) if base else spread * noise
        out[name] = jnp.asarray(drawn.astype(out[name].dtype))
    for name, factor in factors.items():
        out[name] = (out[name] * factor).astype(out[name].dtype)
    return out
```

```python
from contextlib import ExitStack

import concourse.bass as bass
from concourse import mybir

F32 = mybir.dt.float32
F32R = mybir.dt.float32r
BF16 = mybir.dt.bfloat16
I32 = mybir.dt.int32
ALU = mybir.AluOpType
ACT = mybir.ActivationFunctionType
AX_X = mybir.AxisListType.X

P = 128
NEG = -1e30
EPS = 1e-5
HEADS, WINDOW, PREFIX = 16, 256, 16
RSQRT_MAGIC = 0x5F3759DF
FAR, MID, DIAG = 0, 1, 2

SPANS = {
    "V1": (0, 3), "OP0": (3, 6), "OP1": (6, 9), "T1a": (9, 10), "T1b": (10, 11),
    "QK0": (11, 13.5), "QK1": (13.5, 16), "QK2": (16, 18.5), "QK3": (18.5, 21), "T2a": (21, 22), "T2b": (22, 23),
    "UP": (23, 24), "V2": (24, 27), "G": (27, 29.5), "DN0": (30, 31), "DN1": (31, 32),
}
DENSE = list(SPANS)
ATOMS = {"T1a": 1, "T1b": 1, "T2a": 1, "T2b": 1, "DN0": 1, "DN1": 1, "V1": 4, "V2": 4, "OP0": 4, "OP1": 4,
         "UP": 4, "G": 8, "QK0": 8, "QK1": 8, "QK2": 8, "QK3": 8}
PE_SLOTS = {}
for name, (first, end) in SPANS.items():
    for atom in range(ATOMS[name]):
        PE_SLOTS.setdefault(int(first + (end - first) * atom / ATOMS[name]), []).append((name, atom))
ACT_SLOTS = {3: ["V1"], 9: ["T1a"], 10: ["T1b"], 14: ["QK0"], 16: ["QK1"], 19: ["QK2"], 21: ["QK3", "T2a"], 22: ["T2b"],
             25: ["R0", "R1"], 26: ["R2", "R3"], 27: ["R4", "V2", "R5"], 28: ["R6", "R7"]}
DVE_SLOTS = {1: ["LN1"], 6: ["OP0"], 9: ["OP1"], 14: ["QK0"], 15: ["LN2"], 16: ["QK1"],
             19: ["QK2"], 21: ["QK3"], 24: ["UP"], 29: ["G"], 30: ["DN0"], 31: ["DN1"]}
ACT_EVACS = (3, 7, 11, 15)

CREDIT_S, CREDIT_PT, CREDIT_PV, CREDIT_O, CREDIT_PACK, CREDIT_ADD, CREDIT_ST, CREDIT_G = 1, 1, 1, 2, 2, 2, 16, 16
LN_DVE, LN_POOL = 8, 14


def attention_block(nc, x, w_qkv_t, w_out_t, win, bin_, w1, b1, w2, b2, wout, bout, c_t, wmod, out):
    NB, S, D = x.shape
    CH = 2 * P
    NC = NB * S // CH
    CB = S // CH
    KD = D // P
    G = HEADS // 4
    DH = D // HEADS
    M = win.shape[1]
    NJ = w1.shape[1] // 2
    LS = 3 * P + PREFIX
    TB = 4 * G * P
    assert 2 * M == P and WINDOW == CH and CB == 8 and DH == 32 and CB % 2 == 0

    x_rows = x.rearrange("b s d -> (b s) d")
    out_rows = out.rearrange("b s d -> (b s) d")

    with ExitStack() as ctx:
        def sb(name, shape, dt=F32):
            return ctx.enter_context(nc.sbuf_tensor(name, shape, dt))

        def sem(name):
            return ctx.enter_context(nc.semaphore(name))

        wqkv = sb("wqkv", [P, KD, 3 * D])
        wo = sb("wo", [P, G, D])
        win2 = sb("win2", [P, KD, P])
        w2d = sb("w2d", [P, NJ, M])
        wout65 = sb("wout65", [M + 1, D])
        small = sb("small", [P, 3 * NJ + 2])
        w1c, b1c, w2c = small[:, 0:NJ], small[:, NJ:2 * NJ], small[:, 2 * NJ:3 * NJ]
        binc, b2c = small[:, 3 * NJ:3 * NJ + 1], small[0:M, 3 * NJ + 1:3 * NJ + 2]
        modt = sb("modt", [P, 4, KD, NB + 2])
        SA, CA, SB_, CB_ = range(4)
        gab = sb("gab", [P, 2, 2, D])
        ident = sb("ident", [P, P])
        identb = sb("identb", [P, P], BF16)
        mask_diag = sb("mask_diag", [P, P], BF16)
        mask_far = sb("mask_far", [P, P], BF16)
        mask_diag0 = sb("mask_diag0", [P, P], BF16)
        mask_far2 = sb("mask_far2", [P, P], BF16)
        mask_mid1 = sb("mask_mid1", [P, P], BF16)
        xin = sb("xin", [P, 2, 2, D])
        x2 = sb("x2", [P, 2, 2, D])
        tmp = sb("tmp", [P, 2, D])
        xn = sb("xn", [P, 2, D])
        stats = sb("stats", [P, 2, 6])
        mv = sb("mv", [P, 2, 2])
        var = sb("var", [P, 2])
        shifted = sb("shifted", [P, 2], I32)
        half_var = sb("half_var", [P, 2])
        c15 = sb("c15", [P, 2])
        rs = sb("rs", [P, 7, 2])
        ht = sb("ht", [P, 2, KD, CH])
        h2t = sb("h2t", [P, KD, CH])
        stg_q = sb("stg_q", [P, 2, 2, G, P], F32R)
        stg_k = sb("stg_k", [P, 2, 2, G, P], F32R)
        tq = [sb(f"tq{i}", [P, 4, G, P], F32R) for i in range(2)]
        tk = sb("tk", [P, 4, 4, G, P], F32R)
        tkp = sb("tkp", [P, 4, G, PREFIX], F32R)
        vring = sb("vring", [P, 4, D])
        vp = sb("vp", [P, G, P])
        probs = sb("probs", [P, 8, LS])
        ppack = sb("ppack", [P, HEADS, PREFIX])
        pts = sb("pts", [P, 8, 3 * P])
        ptp = sb("ptp", [P, 2, P])
        negm = sb("negm", [P, 2, HEADS])
        sums = sb("sums", [P, 2, HEADS])
        rinv = sb("rinv", [P, HEADS])
        rrep = sb("rrep", [P, HEADS, DH])
        rts = sb("rts", [P, G * P])
        ot = sb("ot", [P, 2, G, P])
        st = sb("st", [P, CH])
        relu = sb("relu", [P, NJ, CH])
        gt = sb("gt", [M + 1, CH])
        cs = sb("cs", [P, 4, KD * NB])

        scr_q = nc.dram_tensor("scr_q", (2, 2, DH, 4, G * P), F32)
        scr_k = nc.dram_tensor("scr_k", (2, 3, DH, 4, G * P), F32)
        scr_g = nc.dram_tensor("scr_g", (NB, 2, D), F32)

        def bank(name):
            return ctx.enter_context(nc.psum_tensor(name, [P, 512], F32))

        s_bank = [bank(f"s_bank{i}") for i in range(2)]
        pt_bank = [bank(f"pt_bank{i}") for i in range(2)]
        pv_bank = [bank(f"pv_bank{i}") for i in range(2)]
        d_bank = [bank(f"d_bank{i}") for i in range(2)]

        w_loaded, c_loaded, m_loaded = sem("w_loaded"), sem("c_loaded"), sem("m_loaded")
        const_done, setup_act, setup_dve, setup_pe = sem("const_done"), sem("setup_act"), sem("setup_dve"), sem("setup_pe")
        scr_g_done = sem("scr_g_done")
        x_loaded = [sem(f"x_loaded{i}") for i in range(2)]
        res_loaded = [sem(f"res_loaded{i}") for i in range(2)]
        gates_loaded, vp_loaded, tkp_ready = sem("gates_loaded"), sem("vp_loaded"), sem("tkp_ready")
        ln_dve, ln_pool = sem("ln_dve"), sem("ln_pool")
        dense_ready = [sem(f"dense_ready{i}") for i in range(2)]
        dense_free = [sem(f"dense_free{i}") for i in range(2)]
        high_ready = sem("high_ready")
        scr_written = [sem(f"scr_written{i}") for i in range(2)]
        stack_ready = [sem(f"stack_ready{i}") for i in range(2)]
        s_ready, m_ready, e_ready = sem("s_ready"), sem("m_ready"), sem("e_ready")
        pt_ready = [sem(f"pt_ready{i}") for i in range(2)]
        pt_evac = [sem(f"pt_evac{i}") for i in range(2)]
        pack_done, rr_ready, pv_ready, o_ready = sem("pack_done"), sem("rr_ready"), sem("pv_ready"), sem("o_ready")
        add_done, relu_ready = sem("add_done"), sem("relu_ready")
        stored = [sem(f"stored{i}") for i in range(2)]

        PRO = [4, 3]

        class Step:

            def __init__(self, eng, p, k, first, b, bases):
                self.eng, self.p, self.k, self.first, self.b, self.bases = eng, p, k, first, b, bases

            def n(self, per, i):
                return self.base(2 * per) + (per * self.k + i)

            def base(self, per):
                if isinstance(self.p, int):
                    return self.p * per
                if per not in self.bases:
                    self.bases[per] = self.eng.snap(self.p * per)
                return self.bases[per]

            def item(self, name):
                i = DENSE.index(name)
                return (i + 1) % 2, self.n(8, PRO[(i + 1) % 2] + i // 2)

            def wait_item_bank(self, name):
                bk, v = self.item(name)
                self.eng.wait_ge(dense_free[bk], v)
                return d_bank[bk]

            def ready(self, name):
                bk, v = self.item(name)
                return dense_ready[bk], v + 1

            def wait_item(self, name):
                bk, v = self.item(name)
                self.eng.wait_ge(dense_ready[bk], v + 1)
                return d_bank[bk]

            def wait_taken(self, name):
                bk, v = self.item(name)
                self.eng.wait_ge(dense_free[bk], v + 1)

            def d_col(self):
                if self.first or self.k == 0:
                    return self.b + 1
                return (self.p * 2 + 2) // CB + 1

            def o_col(self):
                return self.b if self.first and self.k == 0 else self.b + 1

        def norm_val(ln, per, i):
            return ln * per + i if isinstance(ln, int) else ln[0].n(2 * per, ln[1] * per + i)

        def wait_apart(eng, *waits):
            waits = [(s_, v if isinstance(v, int) else eng.to_reg(v)) for s_, v in waits]
            eng.wait_ge(setup_dve, SETUP_DVE)
            for s_, v in waits:
                eng.wait_ge(s_, v)

        def run(eng, step):
            with eng.Fori(0, NB) as b:
                p0 = eng.snap(b * (CB // 2))
                bases = {}
                for k in range(2):
                    step(Step(eng, p0, k, True, b, bases))
                with eng.Fori(1, CB // 2) as i:
                    p = eng.snap(p0 + i)
                    bases = {}
                    for k in range(2):
                        step(Step(eng, p, k, False, b, bases))

        def roles(st_, tile):
            if st_.first and st_.k == 0:
                return [DIAG] if tile == 0 else [MID, DIAG]
            return [FAR, MID, DIAG]

        mod_bufs = [
            relu[:, :, :].rearrange("p a b -> p (a b)").rearrange("p (k n) -> p k n", k=KD),
            x2[:, :, :, :].rearrange("p a b n -> p (a b) n"),
            vring[:, :, :],
            probs[:, :, :].rearrange("p a n -> p (a n)")[:, 0:KD * D].rearrange("p (k n) -> p k n", k=KD),
            ht[:, :, :, :].rearrange("p a k n -> p (a k n)").rearrange("p (k n) -> p k n", k=KD),
            pts[:, :, :].rearrange("p a n -> p (a n)")[:, 0:KD * D].rearrange("p (k n) -> p k n", k=KD),
        ]
        gate_rows = [tmp[0:NB, i, :] for i in range(2)]
        SETUP_SILU, SETUP_GATES, SETUP_DVE = 4, 14, 21
        SETUP_PE = 6
        W_LOADS = 15
        CONST = 20

        EPI = ["OP0", "OP1", "T2a", "T2b", "UP", "G", "DN0", "DN1"]

        def epi_item(name):
            i = EPI.index(name)
            return (i + 1) % 2, 8 * NC + PRO[(i + 1) % 2] + i // 2

        def epi_ready(name):
            bk, v = epi_item(name)
            return dense_ready[bk], v + 1

        def epi_taken(name):
            bk, v = epi_item(name)
            return dense_free[bk], v + 1

        block = ctx.enter_context(nc.Block())

        @block.sync
        def _(sp):
            def stack(t_par, ring, written):
                for v in range(2):
                    for s_, scr, at in ((stg_q, scr_q, [v]), (stg_k, scr_k, [0, 2] if v == 0 else [1])):
                        for a in at:
                            sp.dma_start(scr[t_par, a].rearrange("d j n -> j d n"),
                                         s_[:, ring % 2, v, :, :].bitcast(F32)).then_inc(scr_written[t_par], 16)
                sp.wait_ge(scr_written[t_par], written)
                n = 4 * G * P
                twice = bass.AP(tensor=scr_q, offset=t_par * 2 * DH * n, ap=[[0, 2], [n, 2 * DH], [1, n]])
                sp.dma_start(tq[t_par][:, :, :, :].bitcast(F32), twice).then_inc(stack_ready[t_par], 16)
                turned = bass.AP(tensor=scr_k, offset=t_par * 3 * DH * n, ap=[[DH * n, 2], [n, 2 * DH], [1, n]])
                sp.dma_start(tk[:, ring, :, :, :].bitcast(F32), turned).then_inc(stack_ready[t_par], 16)

            sp.dma_start(cs[:, 0, :].rearrange("p (k b) -> p k b", k=KD),
                         c_t.rearrange("(k p) b -> p k b", p=P)).then_inc(c_loaded, 16)
            wm = wmod.rearrange("(k p) n -> p k n", p=P)
            for v, buf in enumerate(mod_bufs):
                sp.dma_start(buf, wm[:, :, v * D:(v + 1) * D]).then_inc(m_loaded, 16)
            for i in range(2):
                sp.dma_start(xin[:, i, :, :], x_rows[i * CH:(i + 1) * CH, :].rearrange("(t p) d -> p t d", p=P)).then_inc(x_loaded[i], 16)
            sp.dma_start(wqkv[:, :, :], w_qkv_t.rearrange("(k p) n -> p k n", p=P)).then_inc(w_loaded, 16)
            sp.dma_start(wo[:, :, :], w_out_t.rearrange("(k p) n -> p k n", p=P)).then_inc(w_loaded, 16)
            for i in range(2):
                rows = slice(i * M, (i + 1) * M)
                cols = slice(i * NJ, (i + 1) * NJ)
                sp.dma_start(win2[:, :, rows], win.rearrange("(k p) n -> p k n", p=P)).then_inc(w_loaded, 16)
                sp.dma_start(w1c[rows, :], w1[:, cols]).then_inc(w_loaded, 16)
                sp.dma_start(b1c[rows, :], b1[:, cols]).then_inc(w_loaded, 16)
                sp.dma_start(w2c[rows, :], w2[:, cols]).then_inc(w_loaded, 16)
                sp.dma_start(binc[rows, :], bin_.rearrange("(m a) -> m a", a=1)).then_inc(w_loaded, 16)
            sp.dma_start(b2c, b2.rearrange("(m a) -> m a", a=1)).then_inc(w_loaded, 16)
            sp.dma_start(wout65[0:M, :], wout).then_inc(w_loaded, 16)
            sp.dma_start(wout65[M:M + 1, :], bout.rearrange("(a n) -> a n", a=1)).then_inc(w_loaded, 16)
            sp.wait_ge(setup_dve, SETUP_GATES)
            sp.wait_ge(gates_loaded, CREDIT_G)
            for i in range(2):
                sp.dma_start(scr_g[:, i, :], gate_rows[i]).then_inc(scr_g_done, 16)
            sp.wait_ge(setup_pe, SETUP_PE)
            sp.dma_start(x2[:, 1, :, :], x_rows[0:CH, :].rearrange("(t p) d -> p t d", p=P)).then_inc(res_loaded[1], 16)
            sp.wait_ge(dense_free[0], 3)
            sp.wait_ge(dense_free[1], 3)
            sp.wait_ge(scr_g_done, 32)
            stack(0, 0, 80)

            def step(s):
                def value(v):
                    return sp.to_reg(v)

                scored, staged_b = value(s.n(32, CREDIT_S)), value(s.n(80, 80))
                normalized = value(s.n(2 * LN_POOL, LN_POOL))
                rows2 = sp.snap((s.p * 2 + (s.k + 2)) % NC * CH)
                left, rows0 = value(s.base(16) + (16 * s.k + CREDIT_ST)), sp.snap((s.p * 2 + s.k) * CH)
                qk2, qk3 = (value(s.item(name)[1] + 1) for name in ("QK2", "QK3"))
                scored_a, staged_a = value(s.n(32, HEADS + CREDIT_S)), value(s.n(80, 160))
                summed, rows1 = value(s.n(4, 4 + CREDIT_ADD)), sp.snap((s.p * 2 + (s.k + NC - 1)) % NC * CH)
                if s.first and s.k == 0:
                    attended, free0, free1 = value(s.n(2, CREDIT_PV)), value(s.n(8, PRO[0])), value(s.n(8, PRO[1]))
                    row = scr_g[s.b, :, :].rearrange("a n -> (a n)").rearrange("(o n) -> o n", o=1)
                    sp.wait_ge(pv_ready, attended)
                    sp.wait_ge(dense_free[0], free0)
                    sp.wait_ge(dense_free[1], free1)
                    for h in range(HEADS):
                        r, q = (h % 8) * PREFIX, (h % 4) * DH
                        sp.dma_start(vp[r:r + PREFIX, h // 4, q:q + DH],
                                     vring[0:PREFIX, 0, h * DH:(h + 1) * DH]).then_inc(vp_loaded, 16)
                    sp.dma_start(gab[:, (s.b + 1) % 2, :, :].rearrange("p a n -> p (a n)"),
                                 row.to_broadcast([P, 2 * D])).then_inc(gates_loaded, 16)
                sp.wait_ge(s_ready, scored)
                stack(1, 2 * s.k + 1, staged_b)
                sp.wait_ge(ln_pool, normalized)
                sp.dma_start(xin[:, s.k, :, :], x_rows[bass.ds(rows2, CH), :].rearrange("(t p) d -> p t d", p=P)).then_inc(x_loaded[s.k], 16)
                sp.wait_ge(stored[s.k], left)
                sp.dma_start(x2[:, s.k, :, :], x_rows[bass.ds(rows0, CH), :].rearrange("(t p) d -> p t d", p=P)).then_inc(res_loaded[s.k], 16)
                sp.wait_ge(dense_free[s.item("QK2")[0]], qk2)
                sp.wait_ge(dense_free[s.item("QK3")[0]], qk3)
                sp.wait_ge(s_ready, scored_a)
                stack(0, (2 * s.k + 2) % 4, staged_a)
                sp.wait_ge(add_done, summed)
                sp.dma_start(out_rows[bass.ds(rows1, CH), :].rearrange("(t p) d -> p t d", p=P),
                             x2[:, (s.k + 1) % 2, :, :]).then_inc(stored[(s.k + 1) % 2], 16)

            run(sp, step)
            sp.wait_ge(add_done, 4 * NC + 4 + CREDIT_ADD)
            sp.dma_start(out_rows[(NC - 1) * CH:NC * CH, :].rearrange("(t p) d -> p t d", p=P),
                         x2[:, 1, :, :]).then_inc(stored[1], 16)
            sp.wait_ge(stored[0], CREDIT_ST + 16 * (NC // 2))
            sp.wait_ge(stored[1], CREDIT_ST + 16 * (NC // 2 + 1))
            for i in range(2):
                sp.wait_ge(stack_ready[i], 32 * (NC + 1 - i))
                sp.wait_ge(x_loaded[i], 16 * (NC // 2 + 1))

        @block.gpsimd
        def _(pool):
            def build(mask, *conditions):
                pool.memset(mask[:, :], 0.0).then_inc(const_done, 1)
                n[0] += 1
                for base, per_q, per_k in conditions:
                    pool.wait_ge(const_done, n[0])
                    pool.affine_select(out=mask[:, :], in_=mask[:, :], compare_op=ALU.is_ge, fill=NEG, base=base,
                                       pattern=[[per_k, P]], channel_multiplier=per_q).then_inc(const_done, 1)
                    n[0] += 1

            n = [0]
            for m in (ident, identb):
                pool.memset(m[:, :], 0.0).then_inc(const_done, 1)
                n[0] += 1
                pool.wait_ge(const_done, n[0])
                pool.affine_select(out=m[:, :], in_=m[:, :], compare_op=ALU.not_equal, fill=1.0, base=0,
                                   pattern=[[-1, P]], channel_multiplier=1).then_inc(const_done, 1)
                n[0] += 1
            build(mask_diag, (0, 1, -1))
            build(mask_far, (-1, -1, 1))
            build(mask_diag0, (0, 1, -1), (-PREFIX, 0, 1))
            build(mask_far2, (-1, -1, 1), (-PREFIX, 0, 1))
            build(mask_mid1, (-PREFIX, 0, 1))
            for i, (s_, v) in enumerate(((pack_done, CREDIT_PACK), (add_done, CREDIT_ADD),
                                         (stored[0], CREDIT_ST), (stored[1], CREDIT_ST))):
                pool.memset(ppack[:, i, :], 0.0).then_inc(s_, v)
            pool.memset(vp[:, :, :], 0.0).then_inc(const_done, 1)
            pool.memset(gab[:, :, :, :], 0.0).then_inc(gates_loaded, CREDIT_G)
            pool.memset(c15[:, :], 1.5).then_inc(const_done, 1)
            pool.memset(ot[:, :, :, :], 0.0).then_inc(const_done, 1)
            pool.memset(modt[:, :, :, :], 0.0).then_inc(const_done, 1)
            assert n[0] + 4 == CONST

            def norm(ln, src, xn_read=None):
                def so_far(i):
                    return norm_val(ln, LN_POOL, i)

                pool.wait_ge(ln_dve, norm_val(ln, LN_DVE, LN_DVE))
                y = rs[:, 0, :]
                i = 0
                for it in range(3):
                    a, b = rs[:, 2 * it + 1, :], rs[:, 2 * it + 2, :]
                    if i:
                        pool.wait_ge(ln_pool, so_far(i))
                    pool.tensor_tensor(a, y, y, ALU.mult).then_inc(ln_pool, 1)
                    pool.wait_ge(ln_pool, so_far(i + 1))
                    pool.tensor_tensor(b, a, half_var[:, :], ALU.mult).then_inc(ln_pool, 1)
                    pool.wait_ge(ln_pool, so_far(i + 2))
                    pool.tensor_tensor(a, b, c15[:, :], ALU.add).then_inc(ln_pool, 1)
                    pool.wait_ge(ln_pool, so_far(i + 3))
                    pool.tensor_tensor(b, a, y, ALU.mult).then_inc(ln_pool, 1)
                    y = b
                    i += 4
                wait_apart(pool, (ln_pool, so_far(i)), *([xn_read] if xn_read else []))
                for t in range(2):
                    pool.tensor_scalar(xn[:, t, :], src[:, t, :], mv[:, t, 0:1], y[:, t:t + 1],
                                       ALU.subtract, ALU.mult).then_inc(ln_pool, 1)

            norm(0, xin[:, 0, :, :])

            def pack(s, tile, g):
                wait_apart(pool, (e_ready, s.n(32, 16 * tile + 4 * g + 4)))
                pool.tensor_copy(ppack[:, 4 * g:4 * g + 4, :],
                                 probs[:, (4 * g) % 8:(4 * g) % 8 + 4, 3 * P:LS]).then_inc(pack_done, 1)

            def add(s, i):
                o, t = (s.k + 1) % 2, i % 2
                if i == 0:
                    pool.wait_ge(res_loaded[o], s.base(16) + 16)
                pool.tensor_tensor(x2[:, o, t, :], tmp[:, t, :], x2[:, o, t, :], ALU.add).then_inc(add_done, 1)

            def o_sum(s, i):
                s.wait_taken(("OP0", "OP1", "DN0", "DN1")[i])
                add(s, i)

            def step(s):
                norm((s, 1), xin[:, (s.k + 1) % 2, :, :])
                pack(s, 0, 0)
                o_sum(s, 0)
                pack(s, 0, 1)
                o_sum(s, 1)
                pack(s, 0, 2)
                pack(s, 0, 3)
                norm((s, 2), x2[:, (s.k + 1) % 2, :, :], s.ready("T1b"))
                for g in range(4):
                    pack(s, 1, g)
                o_sum(s, 2)
                o_sum(s, 3)

            run(pool, step)
            last = Step(pool, NC // 2, 0, False, NB - 1, {})
            for i, name in enumerate(("OP0", "OP1", "DN0", "DN1")):
                pool.wait_ge(*epi_taken(name))
                add(last, i)
                if i == 1:
                    norm((last, 1), x2[:, 1, :, :])

        @block.scalar
        def _(act):
            act.wait_ge(c_loaded, 16)
            act.activation(cs[:, 1, :], cs[:, 0, :], ACT.Exp, scale=-1.0).then_inc(setup_act, 1)

            def modulate(item_bank, dst, half, shift, scale, col, free):
                for i in range(2):
                    kd = 2 * half + i
                    ins = act.activation(dst[:, kd, :], item_bank[:, i * CH:(i + 1) * CH], ACT.Identity,
                                         bias=modt[:, shift, kd, bass.ds(col, 1)],
                                         scale=modt[:, scale, kd, bass.ds(col, 1)])
                ins.then_inc(free, 1)

            def high(bk_tile, q):
                s_ = stg_q if q < 2 else stg_k
                g = 2 * (q % 2)
                act.activation(s_[:, :, 0, g:g + 2, :].rearrange("p t g n -> p g t n"),
                               bk_tile[:, :].rearrange("p (g t n) -> p g t n", g=2, t=2), ACT.Copy).then_inc(high_ready, 1)

            act.wait_ge(setup_dve, SETUP_DVE)
            for half in range(2):
                act.wait_ge(dense_ready[half], 1)
                modulate(d_bank[half], ht[:, 0, :, :], half, SA, CA, 1, dense_free[half])
            for q in range(4):
                act.wait_ge(dense_ready[q % 2], 2 + q // 2)
                high(d_bank[q % 2], q)
            act.wait_ge(dense_ready[0], 4)
            act.activation(vring[:, 0, :], d_bank[0][:, :], ACT.Copy).then_inc(dense_free[0], 1)

            def exp(s, h):
                tile, h = divmod(h, 16)
                lo = roles(s, tile)[0] * P
                act.wait_ge(m_ready, s.n(32, 16 * tile + h + 1))
                if h % 4 == 0:
                    act.wait_ge(pack_done, s.n(8, 4 * tile + h // 4 - 1 + CREDIT_PACK))
                act.activation(probs[:, h % 8, lo:LS], s_bank[h % 2][:, lo:LS], ACT.Exp,
                               bias=negm[:, tile, h:h + 1], accum_out=sums[:, tile, h:h + 1]).then_inc(e_ready, 1)

            def job(s, name):
                if name in ("T1a", "T1b", "T2a", "T2b"):
                    d_col, o_col = act.snap(s.d_col()), act.snap(s.o_col())
                    bk = d_bank[s.item(name)[0]]
                    wait_apart(act, s.ready(name))
                    free = dense_free[s.item(name)[0]]
                    if name[1] == "1":
                        modulate(bk, ht[:, (s.k + 1) % 2, :, :], "ab".index(name[2]), SA, CA, d_col, free)
                    else:
                        modulate(bk, h2t, "ab".index(name[2]), SB_, CB_, o_col, free)
                elif name in ("V1", "V2"):
                    bk = s.wait_item(name)
                    slot = (2 * s.k + int(name[1])) % 4
                    act.wait_ge(pv_ready, s.n(2, int(name[1]) - 1 + CREDIT_PV))
                    act.activation(vring[:, slot, :], bk[:, :], ACT.Copy).then_inc(dense_free[s.item(name)[0]], 1)
                elif name.startswith("QK"):
                    bk = s.wait_item(name)
                    if name == "QK0":
                        act.wait_ge(scr_written[1], s.n(80, 80))
                        act.wait_ge(scr_written[0], s.n(80, 80))
                    high(bk, int(name[2]))
                elif name[0] == "R":
                    j = int(name[1])
                    if j == 0:
                        s.wait_taken("UP")
                    act.activation(relu[:, j, :], st[:, :], ACT.Relu, bias=b1c[:, j:j + 1],
                                   scale=w1c[:, j:j + 1]).then_inc(relu_ready, 1)

            def evac(s, tile, h):
                lo = roles(s, tile)[0] * P
                act.wait_ge(pt_ready[h % 2], s.n(18, 9 * tile + h // 2 + 1))
                act.activation(pts[:, h % 8, lo:3 * P], pt_bank[h % 2][:, lo:3 * P], ACT.Copy).then_inc(pt_evac[h % 2], 1)

            def tail(s, tile):
                act.wait_ge(pt_ready[0], s.n(18, 9 * tile + 9))
                act.activation(ptp[:, :, :].rearrange("p a n -> p (a n)"), pt_bank[0][:, 0:2 * P], ACT.Copy).then_inc(pt_evac[0], 1)
                act.wait_ge(pt_ready[1], s.n(18, 9 * tile + 9))
                act.activation(rts[:, :], pt_bank[1][:, :], ACT.Copy).then_inc(pt_evac[1], 1)

            def step(s):
                for i in range(32):
                    exp(s, i)
                    if i % 16 and (i - 1) % 16 in ACT_EVACS:
                        evac(s, i // 16, (i - 1) % 16)
                    if i == 16:
                        evac(s, 0, 15)
                        tail(s, 0)
                    for name in ACT_SLOTS.get(i, ()):
                        job(s, name)
                evac(s, 1, 15)
                tail(s, 1)

            run(act, step)
            for half, name in enumerate(("T2a", "T2b")):
                act.wait_ge(*epi_ready(name))
                bk = epi_item(name)[0]
                modulate(d_bank[bk], h2t, half, SB_, CB_, NB, dense_free[bk])
            for j in range(NJ):
                if j == 0:
                    act.wait_ge(*epi_taken("UP"))
                act.activation(relu[:, j, :], st[:, :], ACT.Relu, bias=b1c[:, j:j + 1],
                               scale=w1c[:, j:j + 1]).then_inc(relu_ready, 1)

        @block.vector
        def _(dve):
            n = [0]

            def chained(ins):
                n[0] += 1
                ins.then_inc(setup_dve, 1)
                dve.wait_ge(setup_dve, n[0])

            def stats_of(ln, src):
                def so_far(i):
                    return norm_val(ln, LN_DVE, i)

                for t in range(2):
                    dve.bn_stats(stats[:, t, :], src[:, t, :]).then_inc(ln_dve, 1)
                wait_apart(dve, (ln_dve, so_far(2)))
                for t in range(2):
                    dve.bn_aggr(mv[:, t, :], stats[:, t, :]).then_inc(ln_dve, 1)
                dve.wait_ge(ln_dve, so_far(4))
                dve.tensor_scalar(var[:, :], mv[:, :, 1], EPS, None, ALU.add).then_inc(ln_dve, 1)
                dve.wait_ge(ln_dve, so_far(5))
                dve.tensor_scalar(half_var[:, :], var[:, :], -0.5, None, ALU.mult).then_inc(ln_dve, 1)
                dve.tensor_scalar(shifted[:, :], var[:, :].bitcast(I32), 1, None, ALU.logical_shift_right).then_inc(ln_dve, 1)
                dve.wait_ge(ln_dve, so_far(7))
                dve.tensor_scalar(rs[:, 0, :].bitcast(I32), shifted[:, :], -1.0, float(RSQRT_MAGIC), ALU.mult, ALU.add).then_inc(ln_dve, 1)

            def low(bk_tile, q, v, free):
                s_ = stg_q if q < 2 else stg_k
                g = 2 * (q % 2)
                dve.wait_ge(high_ready, v)
                dve.tensor_tensor(s_[:, :, 1, g:g + 2, :].rearrange("p t g n -> p g t n"),
                                  bk_tile[:, :].rearrange("p (g t n) -> p g t n", g=2, t=2),
                                  s_[:, :, 0, g:g + 2, :].rearrange("p t g n -> p g t n").bitcast(F32),
                                  ALU.subtract).then_inc(free, 1)

            chained(dve.memset(gt[M:M + 1, :], 1.0))
            dve.wait_ge(setup_act, 1)
            chained(dve.tensor_scalar(cs[:, 2, :], cs[:, 1, :], 1.0, None, ALU.add))
            chained(dve.reciprocal(cs[:, 1, :], cs[:, 2, :]))
            chained(dve.tensor_tensor(cs[:, 3, :], cs[:, 0, :], cs[:, 1, :], ALU.mult))
            for i in range(2):
                dve.wait_ge(setup_pe, 1 + i)
                g, a, b = gate_rows[i], rts[0:NB, :], rrep[0:NB, :, :].rearrange("p a b -> p (a b)")
                chained(dve.tensor_copy(g, d_bank[i][0:NB, :]))
                chained(dve.scalar_tensor_tensor(out=a, in0=g, scalar=-1.0, in1=g, op0=ALU.mult, op1=ALU.max))
                chained(dve.tensor_scalar(b, g, 0.0, 2.0, ALU.is_ge, ALU.mult))
                chained(dve.tensor_scalar(a, a, 0.25, None, ALU.max))
                chained(dve.scalar_tensor_tensor(out=g, in0=b, scalar=-1.0, in1=a, op0=ALU.add, op1=ALU.mult))
            assert n[0] == SETUP_GATES
            dve.wait_ge(const_done, CONST)
            for v in range(4):
                dve.wait_ge(setup_pe, 3 + v)
                src = s_bank[v % 2] if v < 2 else pt_bank[v % 2]
                chained(dve.tensor_scalar(modt[:, v, :, 1:NB + 1], src[:, 0:KD * NB].rearrange("p (k b) -> p k b", k=KD),
                                          float(v % 2), None, ALU.add))
            dve.wait_ge(w_loaded, 16 * W_LOADS)
            chained(dve.tensor_scalar(wqkv[:, :, 0:D], wqkv[:, :, 0:D], float(DH) ** -0.5, None, ALU.mult))
            for half in range(2):
                rows = slice(half * M, (half + 1) * M)
                for j in range(NJ):
                    ins = dve.tensor_scalar(w2d[rows, j, :], ident[rows, rows], w2c[rows, j:j + 1], None, ALU.mult)
                chained(ins)
            for i, (s_, v) in enumerate(((pt_evac[0], CREDIT_PT), (pt_evac[1], CREDIT_PT), (o_ready, CREDIT_O))):
                dve.memset(sums[:, 0, i:i + 1], 0.0).then_inc(s_, v)
            assert n[0] == SETUP_DVE

            dve.wait_ge(gates_loaded, CREDIT_G)
            dve.wait_ge(x_loaded[0], 16)
            stats_of(0, xin[:, 0, :, :])
            for q in range(4):
                low(d_bank[q % 2], q, q + 1, dense_free[q % 2])

            def rowmax(s, i):
                tile, h = divmod(i, 16)
                lo = roles(s, tile)[0] * P
                dve.wait_ge(s_ready, s.n(32, i + 1 + CREDIT_S))
                dve.tensor_reduce(negm[:, tile, h:h + 1], s_bank[h % 2][:, lo:LS], AX_X, ALU.max,
                                  negate=True).then_inc(m_ready, 1)

            def evac(s, tile, h):
                lo = roles(s, tile)[0] * P
                dve.wait_ge(pt_ready[h % 2], s.n(18, 9 * tile + h // 2 + 1))
                dve.tensor_copy(pts[:, h % 8, lo:3 * P], pt_bank[h % 2][:, lo:3 * P]).then_inc(pt_evac[h % 2], 1)

            def inverse(s, tile):
                dve.wait_ge(e_ready, s.n(32, 16 * tile + 16))
                dve.reciprocal(rinv[:, :], sums[:, tile, :]).then_inc(rr_ready, 1)
                dve.wait_ge(rr_ready, s.n(4, 2 * tile + 1))
                dve.tensor_copy(rrep[:, :, :], rinv[:, :].unsqueeze(2).to_broadcast([P, HEADS, DH])).then_inc(rr_ready, 1)

            def normalize(s, tile):
                dve.wait_ge(pt_evac[1], s.n(18, 9 * tile + 9 + CREDIT_PT))
                dve.wait_ge(pv_ready, s.n(2, tile + 1 + CREDIT_PV))
                dve.tensor_tensor(ot[:, tile, :, :].rearrange("p g n -> p (g n)"), pv_bank[tile][:, :], rts[:, :],
                                  ALU.mult).then_inc(o_ready, 1)

            def gated(i, bk, which, par, free):
                dve.tensor_tensor(tmp[:, i:i + 1, :], bk[:, :].rearrange("p (a n) -> p a n", a=1),
                                  gab[:, bass.ds(par, 1), which, :], ALU.mult).then_inc(free, 1)

            def gate_par(s):
                return dve.snap(s.o_col() % 2)

            def job(s, name):
                o_par = (s.k + 1) % 2
                if name == "LN1":
                    dve.wait_ge(x_loaded[o_par], s.base(16) + 16 * (1 + s.k))
                    dve.wait_ge(ln_pool, s.n(2 * LN_POOL, LN_POOL))
                    stats_of((s, 1), xin[:, o_par, :, :])
                elif name == "LN2":
                    dve.wait_ge(add_done, s.n(4, 2 + CREDIT_ADD))
                    dve.wait_ge(ln_pool, s.n(2 * LN_POOL, 2 * LN_POOL))
                    stats_of((s, 2), x2[:, o_par, :, :])
                elif name in ("OP0", "OP1"):
                    bk = s.wait_item(name)
                    t = int(name[2])
                    if s.first and s.k == 1 and t == 0:
                        dve.wait_ge(gates_loaded, s.b * 16 + (16 + CREDIT_G))
                    dve.wait_ge(add_done, s.n(4, t - 1 + CREDIT_ADD))
                    gated(t, bk, 0, gate_par(s), dense_free[s.item(name)[0]])
                elif name in ("DN0", "DN1"):
                    bk = s.wait_item(name)
                    t = int(name[2])
                    dve.wait_ge(add_done, s.n(4, t + 1 + CREDIT_ADD))
                    gated(t, bk, 1, gate_par(s), dense_free[s.item(name)[0]])
                elif name.startswith("QK"):
                    q = int(name[2])
                    bk, _ = s.item(name)
                    low(d_bank[bk], q, s.n(4, 4 + q + 1), dense_free[bk])
                elif name == "UP":
                    bk = s.wait_item(name)
                    dve.tensor_scalar(st[:, :], bk[:, 0:CH], binc, None, ALU.add).then_inc(dense_free[s.item(name)[0]], 1)
                elif name == "G":
                    bk = s.wait_item(name)
                    dve.tensor_scalar(gt[0:M, :], bk[0:M, 0:CH], b2c, None, ALU.add).then_inc(dense_free[s.item(name)[0]], 1)

            def step(s):
                if s.first and s.k == 0:
                    dve.wait_ge(stack_ready[0], s.base(64) + 32)
                    dve.wait_ge(s_ready, s.n(32, CREDIT_S))
                    dve.tensor_copy(tkp[:, :, :, :], tk[:, 0, :, :, 0:PREFIX].bitcast(F32)).then_inc(tkp_ready, 1)
                rowmax(s, 0)
                for i in range(32):
                    if i % 16 and (i - 1) % 16 not in ACT_EVACS:
                        evac(s, i // 16, (i - 1) % 16)
                    if i == 16:
                        inverse(s, 0)
                    if i < 31:
                        rowmax(s, i + 1)
                    if i == 17:
                        normalize(s, 0)
                    for name in DVE_SLOTS.get(i, ()):
                        job(s, name)
                inverse(s, 1)
                normalize(s, 1)

            run(dve, step)
            last = Step(dve, NC // 2, 0, False, NB - 1, {})

            def epi_gated(name, which):
                t = int(name[2])
                bk, v = epi_item(name)
                dve.wait_ge(dense_ready[bk], v + 1)
                dve.wait_ge(add_done, last.n(4, t - 1 + 2 * which + CREDIT_ADD))
                gated(t, d_bank[bk], which, NB % 2, dense_free[bk])

            epi_gated("OP0", 0)
            epi_gated("OP1", 0)
            dve.wait_ge(add_done, last.n(4, 2 + CREDIT_ADD))
            stats_of((last, 1), x2[:, 1, :, :])
            dve.wait_ge(*epi_ready("UP"))
            bk = epi_item("UP")[0]
            dve.tensor_scalar(st[:, :], d_bank[bk][:, 0:CH], binc, None, ALU.add).then_inc(dense_free[bk], 1)
            dve.wait_ge(*epi_ready("G"))
            bk = epi_item("G")[0]
            dve.tensor_scalar(gt[0:M, :], d_bank[bk][0:M, 0:CH], b2c, None, ALU.add).then_inc(dense_free[bk], 1)
            epi_gated("DN0", 1)
            epi_gated("DN1", 1)

        @block.tensor
        def _(pe):
            def group(out_, pairs, start=True):
                for i, (lhsT, rhs) in enumerate(pairs):
                    ins = pe.matmul(out_, lhsT, rhs, start=start and i == 0, stop=i == len(pairs) - 1)
                return ins

            pe.wait_ge(setup_dve, SETUP_SILU)
            pe.wait_ge(m_loaded, 16 * len(mod_bufs))
            batch_cols = [cs[:, 3, k * NB:(k + 1) * NB] for k in range(KD)]
            for i, v in enumerate((2, 5)):
                group(d_bank[i][0:NB, :], [(batch_cols[k], mod_bufs[v][:, k, :]) for k in range(KD)]).then_inc(setup_pe, 1)
            for i, v in enumerate((0, 1, 3, 4)):
                bank_ = s_bank[i] if i < 2 else pt_bank[i - 2]
                for kd in range(KD):
                    ins = group(bank_[:, kd * NB:(kd + 1) * NB],
                                [(mod_bufs[v][:, k, kd * P:(kd + 1) * P], batch_cols[k]) for k in range(KD)])
                ins.then_inc(setup_pe, 1)

            def transpose_xn(bk, half):
                for i in range(2):
                    for t in range(2):
                        kd = 2 * half + i
                        ins = pe.transpose(bk[:, i * CH + t * P:i * CH + (t + 1) * P],
                                           xn[:, t, kd * P:(kd + 1) * P], ident[:, :])
                return ins

            def project_qk(bk, par, q, atom):
                gi, k = divmod(atom, KD)
                col = (q // 2) * D + (2 * (q % 2) + gi) * P
                return pe.matmul(bk[:, gi * CH:(gi + 1) * CH], wqkv[:, k, col:col + P], ht[:, par, k, :],
                                 start=k == 0, stop=k == KD - 1)

            def project_v(bk, par, t, k):
                return pe.matmul(bk[:, :], ht[:, par, k, t * P:(t + 1) * P], wqkv[:, k, 2 * D:3 * D],
                                 start=k == 0, stop=k == KD - 1)

            def out_project(bk, t, g):
                return pe.matmul(bk[:, :], ot[:, t, g, :], wo[:, g, :], start=g == 0, stop=g == G - 1)

            def ffn_up(bk, k):
                return pe.matmul(bk[:, 0:CH], win2[:, k, :], h2t[:, k, :], start=k == 0, stop=k == KD - 1)

            def ffn_hidden(s, bk, j):
                pe.wait_ge(relu_ready, s.n(NJ, j + 1))
                return pe.matmul(bk[0:M, 0:CH], w2d[:, j, :], relu[:, j, :], start=j == 0, stop=j == NJ - 1)

            def ffn_down(bk, t):
                return pe.matmul(bk[:, :], gt[0:M + 1, t * P:(t + 1) * P], wout65[:, :], start=True, stop=True)

            pe.wait_ge(const_done, CONST)
            pe.wait_ge(w_loaded, 16 * W_LOADS)
            pe.wait_ge(setup_dve, SETUP_DVE)
            pe.wait_ge(ln_pool, LN_POOL)
            pe.transpose(d_bank[0][:, 0:P], ident[:, :], ident[:, :]).then_inc(s_ready, CREDIT_S)
            pe.transpose(d_bank[1][:, 0:P], ident[:, :], ident[:, :]).then_inc(pv_ready, CREDIT_PV)
            for half in range(2):
                transpose_xn(d_bank[half], half).then_inc(dense_ready[half], 1)
            for q in range(4):
                pe.wait_ge(dense_free[q % 2], 1 + q // 2)
                if q == 0:
                    pe.wait_ge(dense_free[1], 1)
                for atom in range(2 * KD):
                    ins = project_qk(d_bank[q % 2], 0, q, atom)
                ins.then_inc(dense_ready[q % 2], 1)
            pe.wait_ge(dense_free[0], 3)
            for k in range(KD):
                ins = project_v(d_bank[0], 0, 0, k)
            ins.then_inc(dense_ready[0], 1)

            def scores(s, i):
                tile, h = divmod(i, 16)
                j, g = h % 4, h // 4
                bk, cur = s_bank[h % 2], 2 * s.k + tile
                if h == 0:
                    pe.wait_ge(stack_ready[tile], s.n(32, 32))
                    if s.first and s.k == 0 and tile == 0:
                        pe.wait_ge(tkp_ready, s.b + 1)
                queries = tq[tile][:, j, g, :]
                seen = roles(s, tile)
                runs, start = [], 0
                for n_ in range(1, len(seen) + 1):
                    slot = (cur - 2 + seen[start]) % 4
                    if n_ == len(seen) or slot + (n_ - start) > 3:
                        runs.append((seen[start], slot, n_ - start))
                        start = n_
                for r, (block_, slot, n_) in enumerate(runs):
                    pe.matmul(bk[:, block_ * P:(block_ + n_) * P], queries, tk[:, slot:slot + n_, j, g, :],
                              start=r == 0, stop=False, skip_group_check=True)
                pe.matmul(bk[:, 3 * P:LS], queries, tkp[:, j, g, :], start=False, stop=False, skip_group_check=True)
                if not s.first or (s.k, tile) == (1, 1):
                    masks = [(FAR, mask_far), (DIAG, mask_diag)]
                else:
                    masks = {(0, 0): [(DIAG, mask_diag0)], (0, 1): [(MID, mask_mid1), (DIAG, mask_diag)],
                             (1, 0): [(FAR, mask_far2), (DIAG, mask_diag)]}[s.k, tile]
                if s.first and s.k == 0 and tile == 0:
                    pe.matmul(bk[:, 3 * P:LS], identb[:, :], mask_diag[:, 0:PREFIX],
                              start=False, stop=False, skip_group_check=True)
                for block_, mask in masks:
                    ins = pe.matmul(bk[:, block_ * P:(block_ + 1) * P], identb[:, :], mask[:, :],
                                    start=False, stop=block_ == DIAG, skip_group_check=True)
                ins.then_inc(s_ready, 1)

            def transpose_probs(s, i):
                tile, h = divmod(i, 16)
                pe.wait_ge(e_ready, s.n(32, i + 1))
                pe.wait_ge(pt_evac[h % 2], s.n(18, 9 * tile + h // 2 + CREDIT_PT))
                for block_ in roles(s, tile):
                    ins = pe.transpose(pt_bank[h % 2][:, block_ * P:(block_ + 1) * P],
                                       probs[:, h % 8, block_ * P:(block_ + 1) * P], ident[:, :])
                ins.then_inc(pt_ready[h % 2], 1)

            def values(s, tile, g):
                for odd in range(2):
                    pe.wait_ge(pt_evac[odd], s.n(18, 9 * tile + 2 * g + 2 + CREDIT_PT))
                for n_, block_ in enumerate(roles(s, tile)):
                    slot = (2 * s.k + tile - 2 + block_) % 4
                    for j in range(4):
                        h = 4 * g + j
                        pe.matmul(pv_bank[tile][j * DH:(j + 1) * DH, g * P:(g + 1) * P],
                                  vring[:, slot, h * DH:(h + 1) * DH], pts[:, h % 8, block_ * P:(block_ + 1) * P],
                                  start=g == 0 and n_ == 0, stop=False, skip_group_check=True)

            def tail_prefix(s, tile):
                pe.wait_ge(pack_done, s.n(8, 4 * tile + 4 + CREDIT_PACK))
                pe.wait_ge(pt_evac[0], s.n(18, 9 * tile + 8 + CREDIT_PT))
                for a in range(2):
                    ins = pe.transpose(pt_bank[0][:, a * P:(a + 1) * P],
                                       ppack[:, 8 * a:8 * a + 8, :].rearrange("p h k -> p (h k)"), ident[:, :])
                ins.then_inc(pt_ready[0], 1)
                values(s, tile, G - 1)

            def tail_values(s, tile):
                pe.wait_ge(rr_ready, s.n(4, 2 * tile + 2))
                pe.wait_ge(pt_evac[1], s.n(18, 9 * tile + 8 + CREDIT_PT))
                for g in range(G):
                    ins = pe.transpose(pt_bank[1][:, g * P:(g + 1) * P],
                                       rrep[:, 4 * g:4 * g + 4, :].rearrange("p h d -> p (h d)"), ident[:, :])
                ins.then_inc(pt_ready[1], 1)
                if s.first and s.k == 0 and tile == 0:
                    pe.wait_ge(vp_loaded, s.b * (16 * HEADS) + 16 * HEADS)
                pe.wait_ge(pt_evac[0], s.n(18, 9 * tile + 9 + CREDIT_PT))
                for g in range(G):
                    ins = pe.matmul(pv_bank[tile][:, g * P:(g + 1) * P], vp[:, g, :], ptp[:, g // 2, :],
                                    start=False, stop=True, skip_group_check=True)
                ins.then_inc(pv_ready, 1)

            def dense(s, name, atom):
                bk, v = s.item(name)
                bank_ = d_bank[bk]
                if atom == 0:
                    pe.wait_ge(dense_free[bk], v)
                    if name == "QK0":
                        s.wait_taken("T1b")
                    elif name == "UP":
                        s.wait_taken("T2b")
                    elif name in ("OP0", "OP1"):
                        pe.wait_ge(o_ready, s.n(2, int(name[2]) - 1 + CREDIT_O))
                    elif name in ("T1a", "T2a"):
                        pe.wait_ge(ln_pool, s.n(2 * LN_POOL, (1 + int(name[1])) * LN_POOL))
                    elif name == "DN0":
                        s.wait_taken("G")
                if name in ("T1a", "T2a", "T1b", "T2b"):
                    ins = transpose_xn(bank_, "ab".index(name[2]))
                elif name.startswith("QK"):
                    ins = project_qk(bank_, (s.k + 1) % 2, int(name[2]), atom)
                elif name == "V1":
                    ins = project_v(bank_, s.k, 1, atom)
                elif name == "V2":
                    ins = project_v(bank_, (s.k + 1) % 2, 0, atom)
                elif name in ("OP0", "OP1"):
                    ins = out_project(bank_, int(name[2]), atom)
                elif name == "UP":
                    ins = ffn_up(bank_, atom)
                elif name == "G":
                    ins = ffn_hidden(s, bank_, atom)
                else:
                    ins = ffn_down(bank_, int(name[2]))
                if atom == ATOMS[name] - 1:
                    ins.then_inc(dense_ready[bk], 1)

            def step(s):
                scores(s, 0)
                for i in range(32):
                    if i < 31:
                        scores(s, i + 1)
                    for name, part in PE_SLOTS.get(i, ()):
                        dense(s, name, part)
                    if i == 16:
                        tail_values(s, 0)
                    transpose_probs(s, i)
                    if i % 4 == 1 and i % 16 > 4:
                        values(s, i // 16, i % 16 // 4 - 1)
                    if i == 15:
                        tail_prefix(s, 0)
                tail_prefix(s, 1)
                tail_values(s, 1)

            run(pe, step)
            last = Step(pe, NC // 2, 0, False, NB - 1, {})
            for name in EPI:
                bk, v = epi_item(name)
                bank_ = d_bank[bk]
                pe.wait_ge(dense_free[bk], v)
                if name in ("OP0", "OP1"):
                    pe.wait_ge(o_ready, last.n(2, int(name[2]) - 1 + CREDIT_O))
                elif name in ("T2a", "T2b"):
                    pe.wait_ge(ln_pool, last.n(2 * LN_POOL, 2 * LN_POOL))
                elif name == "UP":
                    pe.wait_ge(*epi_taken("T2b"))
                elif name == "DN0":
                    pe.wait_ge(*epi_taken("G"))
                for atom in range(ATOMS[name]):
                    if name in ("OP0", "OP1"):
                        ins = out_project(bank_, int(name[2]), atom)
                    elif name in ("T2a", "T2b"):
                        ins = transpose_xn(bank_, "ab".index(name[2]))
                    elif name == "UP":
                        ins = ffn_up(bank_, atom)
                    elif name == "G":
                        ins = ffn_hidden(last, bank_, atom)
                    else:
                        ins = ffn_down(bank_, int(name[2]))
                ins.then_inc(dense_ready[bk], 1)


def kernel(L0_attn_x, L0_attn_w_qkv, L0_attn_w_out, L0_ffn_Win, L0_ffn_bin_, L0_ffn_W1, L0_ffn_b1, L0_ffn_W2,
           L0_ffn_b2, L0_ffn_Wout, L0_ffn_bout, L0_c, L0_wmod):
    import numpy as np
    import concourse.bacc as bacc
    from concourse.bass_utils import run_bass_kernel_spmd

    arrays = {
        "x": np.ascontiguousarray(L0_attn_x),
        "w_qkv_t": np.ascontiguousarray(np.asarray(L0_attn_w_qkv).T),
        "w_out_t": np.ascontiguousarray(np.asarray(L0_attn_w_out).T),
        "win": np.ascontiguousarray(L0_ffn_Win),
        "bin": np.ascontiguousarray(L0_ffn_bin_),
        "w1": np.ascontiguousarray(L0_ffn_W1),
        "b1": np.ascontiguousarray(L0_ffn_b1),
        "w2": np.ascontiguousarray(L0_ffn_W2),
        "b2": np.ascontiguousarray(L0_ffn_b2),
        "wout": np.ascontiguousarray(L0_ffn_Wout),
        "bout": np.ascontiguousarray(L0_ffn_bout),
        "c_t": np.ascontiguousarray(np.asarray(L0_c).T),
        "wmod": np.ascontiguousarray(L0_wmod),
    }
    nc = bacc.Bacc("TRN2", target_bir_lowering=False, num_devices=1)
    args = [nc.dram_tensor("in_" + name, array.shape, F32, kind="ExternalInput").ap() for name, array in arrays.items()]
    out = nc.dram_tensor("out_0", arrays["x"].shape, F32, kind="ExternalOutput").ap()
    attention_block(nc, *args, out)
    result = run_bass_kernel_spmd(nc, [{"in_" + name: array for name, array in arrays.items()}], core_ids=[0])
    return result.results[0]["out_0"]
```

```python
from contextlib import ExitStack

import concourse.bass as bass
from concourse import mybir

F32 = mybir.dt.float32
F32R = mybir.dt.float32r
BF16 = mybir.dt.bfloat16
I32 = mybir.dt.int32
ALU = mybir.AluOpType
ACT = mybir.ActivationFunctionType

P = 128
NEG = -1e30
EPS = 1e-5
HEADS, WINDOW, PREFIX = 16, 256, 16
RSQRT_MAGIC = 0x5F3759DF
FAR, MID, DIAG = 0, 1, 2

SPANS = {
    "OP0": (1, 0, 2.8), "T1a": (0, 1, 2), "OP1": (0, 3, 5.8), "T1b": (1, 4, 5), "QK0": (1, 6.4, 9),
    "QK1": (0, 9, 11.6), "V1": (1, 11.6, 14.4), "T2b": (0, 14, 15), "T2a": (1, 15, 16), "QK2": (0, 16, 19),
    "UP": (1, 17, 18), "QK3": (1, 19.3, 22), "V2": (0, 22, 31.3), "G": (1, 28, 29), "DN0": (1, 31, 32), "DN1": (0, 32, 33),
}
DENSE = list(SPANS)
BANK_ITEMS = [[name for name in DENSE if SPANS[name][0] == bank] for bank in range(2)]
ATOMS = {"T1a": 1, "T1b": 1, "T2a": 1, "T2b": 1, "DN0": 1, "DN1": 1, "V1": 4, "V2": 4, "OP0": 4, "OP1": 4,
         "UP": 4, "G": 1, "QK0": 8, "QK1": 8, "QK2": 8, "QK3": 8}
PE_SLOTS = {}
for name, (_, first, end) in SPANS.items():
    for atom in range(ATOMS[name]):
        PE_SLOTS.setdefault(int(first + (end - first) * atom / ATOMS[name]), []).append((name, atom))
ACT_SLOTS = {2: ["T1a"], 5: ["T1b"], 9: ["QK0"], 12: ["QK1"], 14: ["V1"], 15: ["T2b"], 16: ["T2a"], 19: ["QK2", "R0"],
             20: ["R1"], 21: ["R2"], 22: ["R3", "QK3"], 23: ["R4"], 24: ["R5"], 25: ["R6"], 26: ["R7"], 30: ["V2"]}
DVE_SLOTS = {3: ["OP0"], 6: ["OP1"], 8: ["LN2"], 10: ["QK0"], 12: ["X2"], 13: ["QK1"], 15: ["LN1"], 18: ["UP"], 19: ["X1"],
             20: ["QK2", "A0"], 21: ["A1"], 22: ["A2"], 23: ["QK3", "A3"], 24: ["A4"], 25: ["A5"], 26: ["A6"], 27: ["A7"],
             29: ["G"]}
ACT_EVACS = (3, 5, 7, 9, 11, 13, 15)

CREDIT_S, CREDIT_PT, CREDIT_PV, CREDIT_O, CREDIT_PACK, CREDIT_ADD, CREDIT_ST, CREDIT_G = 1, 1, 1, 2, 2, 2, 16, 16
LN_DVE, LN_POOL = 8, 12


def attention_block(nc, x, w_qkv_t, w_out_t, win, bin_, w1, b1, w2, b2, wout, bout, c_t, wmod, out):
    NB, S, D = x.shape
    CH = 2 * P
    NC = NB * S // CH
    CB = S // CH
    KD = D // P
    G = HEADS // 4
    DH = D // HEADS
    M = win.shape[1]
    NJ = w1.shape[1] // 2
    LS = 3 * P + PREFIX
    TB = 4 * G * P
    assert 2 * M == P and WINDOW == CH and CB == 8 and DH == 32 and CB % 2 == 0

    x_rows = x.rearrange("b s d -> (b s) d")
    out_rows = out.rearrange("b s d -> (b s) d")

    with ExitStack() as ctx:
        def sb(name, shape, dt=F32):
            return ctx.enter_context(nc.sbuf_tensor(name, shape, dt))

        def sem(name):
            return ctx.enter_context(nc.semaphore(name))

        wqkv = sb("wqkv", [P, KD, 3 * D])
        wo = sb("wo", [P, G, D])
        win2 = sb("win2", [P, KD, P])
        fold = sb("fold", [P, M])
        wout65 = sb("wout65", [M + 1, D])
        small = sb("small", [P, 3 * NJ + 2])
        w1c, b1c, w2c = small[:, 0:NJ], small[:, NJ:2 * NJ], small[:, 2 * NJ:3 * NJ]
        binc, b2c = small[:, 3 * NJ:3 * NJ + 1], small[0:M, 3 * NJ + 1:3 * NJ + 2]
        modt = sb("modt", [P, 4, KD, NB + 2])
        SA, CA, SB_, CB_ = range(4)
        gab = sb("gab", [P, 2, 2, D])
        ident = sb("ident", [P, P])
        mask = sb("mask", [P, LS], BF16)
        mask_tile2 = sb("mask_tile2", [P, LS], BF16)
        mask_tile1 = sb("mask_tile1", [P, LS - P], BF16)
        mask_tile0 = sb("mask_tile0", [P, LS - 2 * P], BF16)
        xin = sb("xin", [P, 2, 2, D])
        x2 = sb("x2", [P, 2, 2, D])
        tmp = sb("tmp", [P, 2, D])
        xn = sb("xn", [P, 2, D])
        stats = sb("stats", [P, 2, 6])
        mv = sb("mv", [P, 2, 2])
        var = sb("var", [P, 2])
        shifted = sb("shifted", [P, 2], I32)
        half_var = sb("half_var", [P, 2])
        c15 = sb("c15", [P, 2])
        rs = sb("rs", [P, 7, 2])
        ht = sb("ht", [P, 2, KD, CH])
        h2t = sb("h2t", [P, KD, CH])
        stg_q = sb("stg_q", [P, 2, 2, G, P], F32R)
        stg_k = sb("stg_k", [P, 2, 2, G, P], F32R)
        tq = [sb(f"tq{i}", [P, 4, G, P], F32R) for i in range(2)]
        tk = sb("tk", [P, 4, 4, G, P + PREFIX], F32R)
        vring = sb("vring", [P, 4, D])
        vp = sb("vp", [P, G, P])
        probs = sb("probs", [P, 8, LS])
        ppack = sb("ppack", [P, HEADS, PREFIX])
        pts = sb("pts", [P, 8, 3 * P])
        ptp = sb("ptp", [P, 2, P])
        negm = sb("negm", [P, 2, HEADS])
        sums = sb("sums", [P, 2, HEADS])
        rinv = sb("rinv", [P, HEADS])
        rrep = sb("rrep", [P, HEADS, DH])
        rts = sb("rts", [P, G * P])
        ot = sb("ot", [P, 2, G, P])
        st = sb("st", [P, CH])
        relu = sb("relu", [P, 4, CH])
        acc = sb("acc", [P, CH])
        gt = sb("gt", [M + 1, CH])
        cs = sb("cs", [P, 4, KD * NB])

        scr_q = nc.dram_tensor("scr_q", (2, 2, DH, 4, G * P), F32)
        scr_k = nc.dram_tensor("scr_k", (2, 3, DH, 4, G * P), F32)
        scr_g = nc.dram_tensor("scr_g", (NB, 2, D), F32)

        def bank(name):
            return ctx.enter_context(nc.psum_tensor(name, [P, 512], F32))

        s_bank = [bank(f"s_bank{i}") for i in range(2)]
        pt_bank = [bank(f"pt_bank{i}") for i in range(2)]
        pv_bank = [bank(f"pv_bank{i}") for i in range(2)]
        d_bank = [bank(f"d_bank{i}") for i in range(2)]

        w_loaded, c_loaded, m_loaded = sem("w_loaded"), sem("c_loaded"), sem("m_loaded")
        const_done, setup_act, setup_dve, setup_pe = sem("const_done"), sem("setup_act"), sem("setup_dve"), sem("setup_pe")
        scr_g_done = sem("scr_g_done")
        x_loaded = [sem(f"x_loaded{i}") for i in range(2)]
        res_loaded = [sem(f"res_loaded{i}") for i in range(2)]
        gates_loaded, vp_loaded, prefix_keys_ready = sem("gates_loaded"), sem("vp_loaded"), sem("prefix_keys_ready")
        ln_dve, ln_pool, xn_ready = sem("ln_dve"), sem("ln_pool"), sem("xn_ready")
        dense_ready = [sem(f"dense_ready{i}") for i in range(2)]
        dense_free = [sem(f"dense_free{i}") for i in range(2)]
        high_ready = sem("high_ready")
        scr_written = [sem(f"scr_written{i}") for i in range(2)]
        stack_ready = [sem(f"stack_ready{i}") for i in range(2)]
        s_ready, m_ready, e_ready = sem("s_ready"), sem("m_ready"), sem("e_ready")
        pt_ready = [sem(f"pt_ready{i}") for i in range(2)]
        pt_evac = [sem(f"pt_evac{i}") for i in range(2)]
        pack_done, rr_ready, pv_ready, o_ready = sem("pack_done"), sem("rr_ready"), sem("pv_ready"), sem("o_ready")
        add_done, relu_ready, acc_done = sem("add_done"), sem("relu_ready"), sem("acc_done")
        stored = [sem(f"stored{i}") for i in range(2)]

        PRO = [4, 3]

        class Step:

            def __init__(self, eng, p, k, first, b, bases):
                self.eng, self.p, self.k, self.first, self.b, self.bases = eng, p, k, first, b, bases

            def n(self, per, i):
                return self.base(2 * per) + (per * self.k + i)

            def base(self, per):
                if isinstance(self.p, int):
                    return self.p * per
                if per not in self.bases:
                    self.bases[per] = self.eng.snap(self.p * per)
                return self.bases[per]

            def item(self, name):
                bk = SPANS[name][0]
                per = len(BANK_ITEMS[bk])
                return bk, self.n(per, PRO[bk] + BANK_ITEMS[bk].index(name))

            def ready(self, name):
                bk, v = self.item(name)
                return dense_ready[bk], v + 1

            def wait_item(self, name):
                bk, v = self.item(name)
                self.eng.wait_ge(dense_ready[bk], v + 1)
                return d_bank[bk]

            def wait_taken(self, name):
                bk, v = self.item(name)
                self.eng.wait_ge(dense_free[bk], v + 1)

            def d_col(self):
                if self.first or self.k == 0:
                    return self.b + 1
                return (self.p * 2 + 2) // CB + 1

            def o_col(self):
                return self.b if self.first and self.k == 0 else self.b + 1

        def norm_val(ln, per, i):
            return ln * per + i if isinstance(ln, int) else ln[0].n(2 * per, ln[1] * per + i)

        def wait_apart(eng, *waits):
            waits = [(s_, v if isinstance(v, int) else eng.to_reg(v)) for s_, v in waits]
            eng.wait_ge(setup_dve, SETUP_DVE)
            for s_, v in waits:
                eng.wait_ge(s_, v)

        def run(eng, step):
            with eng.Fori(0, NB) as b:
                p0 = eng.snap(b * (CB // 2))
                bases = {}
                for k in range(2):
                    step(Step(eng, p0, k, True, b, bases))
                with eng.Fori(1, CB // 2) as i:
                    p = eng.snap(p0 + i)
                    bases = {}
                    for k in range(2):
                        step(Step(eng, p, k, False, b, bases))

        def roles(st_, tile):
            if st_.first and st_.k == 0:
                return [DIAG] if tile == 0 else [MID, DIAG]
            return [FAR, MID, DIAG]

        mod_bufs = [
            wo[:, :, :],
            x2[:, :, :, :].rearrange("p a b n -> p (a b) n"),
            vring[:, :, :],
            probs[:, :, :].rearrange("p a n -> p (a n)")[:, 0:KD * D].rearrange("p (k n) -> p k n", k=KD),
            ht[:, :, :, :].rearrange("p a k n -> p (a k n)").rearrange("p (k n) -> p k n", k=KD),
            pts[:, :, :].rearrange("p a n -> p (a n)")[:, 0:KD * D].rearrange("p (k n) -> p k n", k=KD),
        ]
        gate_rows = [tmp[0:NB, i, :] for i in range(2)]
        SETUP_SILU, SETUP_GATES, SETUP_DVE = 4, 14, 21
        SETUP_PE = 6
        W_LOADS = 15
        CONST = 20

        EPI = ["OP0", "OP1", "T2a", "T2b", "UP", "G", "DN0", "DN1"]

        def epi_item(name):
            i = EPI.index(name)
            return (i + 1) % 2, len(BANK_ITEMS[(i + 1) % 2]) * NC + PRO[(i + 1) % 2] + i // 2

        def epi_ready(name):
            bk, v = epi_item(name)
            return dense_ready[bk], v + 1

        def epi_taken(name):
            bk, v = epi_item(name)
            return dense_free[bk], v + 1

        block = ctx.enter_context(nc.Block())

        @block.sync
        def _(sp):
            def stage_out(t_par, s_, scr):
                for v in range(2):
                    for a in ([v] if scr is scr_q else ([0, 2], [1])[v]):
                        sp.dma_start(scr[t_par, a].rearrange("d j n -> j d n"),
                                     s_[:, t_par, v, :, :].bitcast(F32)).then_inc(scr_written[t_par], 16)

            def stack_in(t_par, ring, written):
                sp.wait_ge(scr_written[t_par], written)
                n = 4 * G * P
                twice = bass.AP(tensor=scr_q, offset=t_par * 2 * DH * n, ap=[[0, 2], [n, 2 * DH], [1, n]])
                sp.dma_start(tq[t_par][:, :, :, :].bitcast(F32), twice).then_inc(stack_ready[t_par], 16)
                turned = bass.AP(tensor=scr_k, offset=t_par * 3 * DH * n,
                                 ap=[[DH * n, 2], [n, 2 * DH], [P, 4 * G], [1, P]])
                sp.dma_start(tk[:, ring, :, :, 0:P].rearrange("p j g n -> p (j g) n").bitcast(F32), turned).then_inc(stack_ready[t_par], 16)

            sp.dma_start(cs[:, 0, :].rearrange("p (k b) -> p k b", k=KD),
                         c_t.rearrange("(k p) b -> p k b", p=P)).then_inc(c_loaded, 16)
            wm = wmod.rearrange("(k p) n -> p k n", p=P)
            for v, buf in enumerate(mod_bufs):
                sp.dma_start(buf, wm[:, :, v * D:(v + 1) * D]).then_inc(m_loaded, 16)
            for i in range(2):
                sp.dma_start(xin[:, i, :, :], x_rows[i * CH:(i + 1) * CH, :].rearrange("(t p) d -> p t d", p=P)).then_inc(x_loaded[i], 16)
            sp.dma_start(wqkv[:, :, :], w_qkv_t.rearrange("(k p) n -> p k n", p=P)).then_inc(w_loaded, 16)
            for i in range(2):
                rows = slice(i * M, (i + 1) * M)
                cols = slice(i * NJ, (i + 1) * NJ)
                sp.dma_start(win2[:, :, rows], win.rearrange("(k p) n -> p k n", p=P)).then_inc(w_loaded, 16)
                sp.dma_start(w1c[rows, :], w1[:, cols]).then_inc(w_loaded, 16)
                sp.dma_start(b1c[rows, :], b1[:, cols]).then_inc(w_loaded, 16)
                sp.dma_start(w2c[rows, :], w2[:, cols]).then_inc(w_loaded, 16)
                sp.dma_start(binc[rows, :], bin_.rearrange("(m a) -> m a", a=1)).then_inc(w_loaded, 16)
            sp.dma_start(b2c, b2.rearrange("(m a) -> m a", a=1)).then_inc(w_loaded, 16)
            sp.dma_start(wout65[0:M, :], wout).then_inc(w_loaded, 16)
            sp.dma_start(wout65[M:M + 1, :], bout.rearrange("(a n) -> a n", a=1)).then_inc(w_loaded, 16)
            sp.wait_ge(setup_dve, SETUP_GATES)
            sp.wait_ge(gates_loaded, CREDIT_G)
            for i in range(2):
                sp.dma_start(scr_g[:, i, :], gate_rows[i]).then_inc(scr_g_done, 16)
            sp.wait_ge(setup_pe, SETUP_PE)
            sp.dma_start(wo[:, :, :], w_out_t.rearrange("(k p) n -> p k n", p=P)).then_inc(w_loaded, 16)
            sp.dma_start(x2[:, 1, :, :], x_rows[0:CH, :].rearrange("(t p) d -> p t d", p=P)).then_inc(res_loaded[1], 16)
            sp.wait_ge(dense_free[0], 3)
            sp.wait_ge(dense_free[1], 3)
            sp.wait_ge(scr_g_done, 32)
            stage_out(0, stg_q, scr_q)
            stage_out(0, stg_k, scr_k)
            stack_in(0, 0, 80)

            def step(s):
                def value(v):
                    return sp.to_reg(v)

                scored, staged_b = value(s.n(32, CREDIT_S)), value(s.n(80, 80))
                normalized = value(s.n(4, 2))
                rows2 = sp.snap((s.p * 2 + (s.k + 2)) % NC * CH)
                left, rows0 = value(s.base(16) + (16 * s.k + CREDIT_ST)), sp.snap((s.p * 2 + s.k) * CH)
                qk = [value(s.item(f"QK{q}")[1] + 1) for q in range(4)]
                scored_a, staged_a = value(s.n(32, HEADS + CREDIT_S)), value(s.n(80, 160))
                summed, rows1 = value(s.n(4, 4 + CREDIT_ADD)), sp.snap((s.p * 2 + (s.k + NC - 1)) % NC * CH)
                if s.first and s.k == 0:
                    attended, free0, free1 = value(s.n(2, CREDIT_PV)), *(value(s.n(len(BANK_ITEMS[i]), PRO[i])) for i in range(2))
                    row = scr_g[s.b, :, :].rearrange("a n -> (a n)").rearrange("(o n) -> o n", o=1)
                    sp.wait_ge(pv_ready, attended)
                    sp.wait_ge(dense_free[0], free0)
                    sp.wait_ge(dense_free[1], free1)
                    for h in range(HEADS):
                        r, q = (h % 8) * PREFIX, (h % 4) * DH
                        sp.dma_start(vp[r:r + PREFIX, h // 4, q:q + DH],
                                     vring[0:PREFIX, 0, h * DH:(h + 1) * DH]).then_inc(vp_loaded, 16)
                    sp.dma_start(gab[:, (s.b + 1) % 2, :, :].rearrange("p a n -> p (a n)"),
                                 row.to_broadcast([P, 2 * D])).then_inc(gates_loaded, 16)
                sp.wait_ge(s_ready, scored)
                stage_out(1, stg_q, scr_q)
                stage_out(1, stg_k, scr_k)
                stack_in(1, 2 * s.k + 1, staged_b)
                sp.wait_ge(xn_ready, normalized)
                sp.dma_start(xin[:, s.k, :, :], x_rows[bass.ds(rows2, CH), :].rearrange("(t p) d -> p t d", p=P)).then_inc(x_loaded[s.k], 16)
                sp.wait_ge(stored[s.k], left)
                sp.dma_start(x2[:, s.k, :, :], x_rows[bass.ds(rows0, CH), :].rearrange("(t p) d -> p t d", p=P)).then_inc(res_loaded[s.k], 16)
                sp.wait_ge(s_ready, scored_a)
                for q in range(4):
                    sp.wait_ge(dense_free[s.item(f"QK{q}")[0]], qk[q])
                    if q % 2:
                        stage_out(0, *((stg_q, scr_q), (stg_k, scr_k))[q // 2])
                stack_in(0, (2 * s.k + 2) % 4, staged_a)
                sp.wait_ge(add_done, summed)
                sp.dma_start(out_rows[bass.ds(rows1, CH), :].rearrange("(t p) d -> p t d", p=P),
                             x2[:, (s.k + 1) % 2, :, :]).then_inc(stored[(s.k + 1) % 2], 16)

            run(sp, step)
            sp.wait_ge(add_done, 4 * NC + 4 + CREDIT_ADD)
            sp.dma_start(out_rows[(NC - 1) * CH:NC * CH, :].rearrange("(t p) d -> p t d", p=P),
                         x2[:, 1, :, :]).then_inc(stored[1], 16)
            sp.wait_ge(stored[0], CREDIT_ST + 16 * (NC // 2))
            sp.wait_ge(stored[1], CREDIT_ST + 16 * (NC // 2 + 1))
            for i in range(2):
                sp.wait_ge(stack_ready[i], 32 * (NC + 1 - i))
                sp.wait_ge(x_loaded[i], 16 * (NC // 2 + 1))

        @block.gpsimd
        def _(pool):
            def build(m, *conditions):
                pool.memset(m[:, :], 0.0).then_inc(const_done, 1)
                n[0] += 1
                for at, width, base, per_q, per_k in conditions:
                    part = m[:, at:at + width]
                    pool.wait_ge(const_done, n[0])
                    pool.affine_select(out=part, in_=part, compare_op=ALU.is_ge, fill=NEG, base=base,
                                       pattern=[[per_k, width]], channel_multiplier=per_q).then_inc(const_done, 1)
                    n[0] += 1

            n = [0]
            pool.memset(ident[:, :], 0.0).then_inc(const_done, 1)
            pool.wait_ge(const_done, 1)
            pool.affine_select(out=ident[:, :], in_=ident[:, :], compare_op=ALU.not_equal, fill=1.0, base=0,
                               pattern=[[-1, P]], channel_multiplier=1).then_inc(const_done, 1)
            n[0] = 2
            build(mask, (0, P, -1, -1, 1), (2 * P, P, 0, 1, -1))
            build(mask_tile2, (0, P, -1, -1, 1), (0, P, -PREFIX, 0, 1), (2 * P, P, 0, 1, -1))
            build(mask_tile1, (0, P, -PREFIX, 0, 1), (P, P, 0, 1, -1))
            build(mask_tile0, (0, P, 0, 1, -1), (0, P, -PREFIX, 0, 1), (P, PREFIX, 0, 1, -1))
            for i, (s_, v) in enumerate(((pack_done, CREDIT_PACK), (add_done, CREDIT_ADD),
                                         (stored[0], CREDIT_ST), (stored[1], CREDIT_ST))):
                pool.memset(ppack[:, i, :], 0.0).then_inc(s_, v)
            pool.memset(vp[:, :, :], 0.0).then_inc(const_done, 1)
            pool.memset(gab[:, :, :, :], 0.0).then_inc(gates_loaded, CREDIT_G)
            pool.memset(c15[:, :], 1.5).then_inc(const_done, 1)
            pool.memset(ot[:, :, :, :], 0.0).then_inc(const_done, 1)
            pool.memset(modt[:, :, :, :], 0.0).then_inc(const_done, 1)
            assert n[0] + 4 == CONST

            def norm(ln):
                def so_far(i):
                    return norm_val(ln, LN_POOL, i)

                pool.wait_ge(ln_dve, norm_val(ln, LN_DVE, LN_DVE))
                y = rs[:, 0, :]
                i = 0
                for it in range(3):
                    a, b = rs[:, 2 * it + 1, :], rs[:, 2 * it + 2, :]
                    if i:
                        pool.wait_ge(ln_pool, so_far(i))
                    pool.tensor_tensor(a, y, y, ALU.mult).then_inc(ln_pool, 1)
                    pool.wait_ge(ln_pool, so_far(i + 1))
                    pool.tensor_tensor(b, a, half_var[:, :], ALU.mult).then_inc(ln_pool, 1)
                    pool.wait_ge(ln_pool, so_far(i + 2))
                    pool.tensor_tensor(a, b, c15[:, :], ALU.add).then_inc(ln_pool, 1)
                    pool.wait_ge(ln_pool, so_far(i + 3))
                    pool.tensor_tensor(b, a, y, ALU.mult).then_inc(ln_pool, 1)
                    y = b
                    i += 4
            norm(0)
            norm(1)

            def pack(s, tile, g):
                wait_apart(pool, (e_ready, s.n(32, 16 * tile + 4 * g + 4)))
                pool.tensor_copy(ppack[:, 4 * g:4 * g + 4, :],
                                 probs[:, (4 * g) % 8:(4 * g) % 8 + 4, 3 * P:LS]).then_inc(pack_done, 1)

            def add(s, i):
                o, t = (s.k + 1) % 2, i % 2
                if i == 0:
                    pool.wait_ge(res_loaded[o], s.base(16) + 16)
                pool.tensor_tensor(x2[:, o, t, :], tmp[:, t, :], x2[:, o, t, :], ALU.add).then_inc(add_done, 1)

            def o_sum(s, i):
                s.wait_taken(("OP0", "OP1", "DN0", "DN1")[i])
                add(s, i)

            def step(s):
                pack(s, 0, 0)
                o_sum(s, 0)
                o_sum(s, 1)
                pack(s, 0, 1)
                norm((s, 2))
                pack(s, 0, 2)
                pack(s, 0, 3)
                for g in range(4):
                    if g == 0:
                        norm((s, 3))
                    pack(s, 1, g)
                o_sum(s, 2)
                o_sum(s, 3)

            run(pool, step)
            last = Step(pool, NC // 2, 0, False, NB - 1, {})
            for i, name in enumerate(("OP0", "OP1", "DN0", "DN1")):
                pool.wait_ge(*epi_taken(name))
                add(last, i)
                if i == 1:
                    norm((last, 2))

        @block.scalar
        def _(act):
            act.wait_ge(c_loaded, 16)
            act.activation(cs[:, 1, :], cs[:, 0, :], ACT.Exp, scale=-1.0).then_inc(setup_act, 1)

            def modulate(item_bank, dst, half, shift, scale, col, free):
                for i in range(2):
                    kd = 2 * half + i
                    ins = act.activation(dst[:, kd, :], item_bank[:, i * CH:(i + 1) * CH], ACT.Identity,
                                         bias=modt[:, shift, kd, bass.ds(col, 1)],
                                         scale=modt[:, scale, kd, bass.ds(col, 1)])
                ins.then_inc(free, 1)

            def high(bk_tile, q):
                s_ = stg_q if q < 2 else stg_k
                g = 2 * (q % 2)
                act.activation(s_[:, :, 0, g:g + 2, :].rearrange("p t g n -> p g t n"),
                               bk_tile[:, :].rearrange("p (g t n) -> p g t n", g=2, t=2), ACT.Copy).then_inc(high_ready, 1)

            act.wait_ge(setup_dve, SETUP_DVE)
            for half in range(2):
                act.wait_ge(dense_ready[half], 1)
                modulate(d_bank[half], ht[:, 0, :, :], half, SA, CA, 1, dense_free[half])
            for q in range(4):
                act.wait_ge(dense_ready[q % 2], 2 + q // 2)
                high(d_bank[q % 2], q)
            act.wait_ge(dense_ready[0], 4)
            act.activation(vring[:, 0, :], d_bank[0][:, :], ACT.Copy).then_inc(dense_free[0], 1)

            def exp(s, h):
                tile, h = divmod(h, 16)
                lo = roles(s, tile)[0] * P
                act.wait_ge(m_ready, s.n(32, 16 * tile + h + 1))
                act.activation(probs[:, h % 8, lo:LS], probs[:, h % 8, lo:LS], ACT.Exp, scale=-1.0,
                               bias=negm[:, tile, h:h + 1], accum_out=sums[:, tile, h:h + 1]).then_inc(e_ready, 1)

            def job(s, name):
                if name in ("T1a", "T1b", "T2a", "T2b"):
                    d_col, o_col = act.snap(s.d_col()), act.snap(s.o_col())
                    bk = d_bank[s.item(name)[0]]
                    wait_apart(act, s.ready(name))
                    free = dense_free[s.item(name)[0]]
                    if name[1] == "1":
                        modulate(bk, ht[:, (s.k + 1) % 2, :, :], "ab".index(name[2]), SA, CA, d_col, free)
                    else:
                        modulate(bk, h2t, "ab".index(name[2]), SB_, CB_, o_col, free)
                elif name in ("V1", "V2"):
                    bk = s.wait_item(name)
                    slot = (2 * s.k + int(name[1])) % 4
                    act.wait_ge(pv_ready, s.n(2, int(name[1]) - 1 + CREDIT_PV))
                    act.activation(vring[:, slot, :], bk[:, :], ACT.Copy).then_inc(dense_free[s.item(name)[0]], 1)
                elif name.startswith("QK"):
                    bk = s.wait_item(name)
                    if name == "QK0":
                        act.wait_ge(scr_written[1], s.n(80, 80))
                        act.wait_ge(scr_written[0], s.n(80, 80))
                    high(bk, int(name[2]))
                elif name[0] == "R":
                    j = int(name[1])
                    if j == 0:
                        s.wait_taken("UP")
                    elif j >= 4:
                        act.wait_ge(acc_done, s.n(NJ, j - 3))
                    act.activation(relu[:, j % 4, :], st[:, :], ACT.Relu, bias=b1c[:, j:j + 1],
                                   scale=w1c[:, j:j + 1]).then_inc(relu_ready, 1)

            def evac(s, tile, h):
                lo = roles(s, tile)[0] * P
                act.wait_ge(pt_ready[h % 2], s.n(18, 9 * tile + h // 2 + 1))
                act.activation(pts[:, h % 8, lo:3 * P], pt_bank[h % 2][:, lo:3 * P], ACT.Copy).then_inc(pt_evac[h % 2], 1)

            def tail(s, tile):
                act.wait_ge(pt_ready[0], s.n(18, 9 * tile + 9))
                act.activation(ptp[:, :, :].rearrange("p a n -> p (a n)"), pt_bank[0][:, 0:2 * P], ACT.Copy).then_inc(pt_evac[0], 1)
                act.wait_ge(pt_ready[1], s.n(18, 9 * tile + 9))
                act.activation(rts[:, :], pt_bank[1][:, :], ACT.Copy).then_inc(pt_evac[1], 1)

            def step(s):
                for i in range(32):
                    exp(s, i)
                    if i % 16 and (i - 1) % 16 in ACT_EVACS:
                        evac(s, i // 16, (i - 1) % 16)
                    if i == 16:
                        evac(s, 0, 15)
                        tail(s, 0)
                    for name in ACT_SLOTS.get(i, ()):
                        job(s, name)
                evac(s, 1, 15)
                tail(s, 1)

            run(act, step)
            for half, name in enumerate(("T2a", "T2b")):
                act.wait_ge(*epi_ready(name))
                bk = epi_item(name)[0]
                modulate(d_bank[bk], h2t, half, SB_, CB_, NB, dense_free[bk])
            for j in range(NJ):
                if j == 0:
                    act.wait_ge(*epi_taken("UP"))
                elif j >= 4:
                    act.wait_ge(acc_done, NC * NJ + j - 3)
                act.activation(relu[:, j % 4, :], st[:, :], ACT.Relu, bias=b1c[:, j:j + 1],
                               scale=w1c[:, j:j + 1]).then_inc(relu_ready, 1)

        @block.vector
        def _(dve):
            n = [0]

            def chained(ins):
                n[0] += 1
                ins.then_inc(setup_dve, 1)
                dve.wait_ge(setup_dve, n[0])

            def stats_of(ln, src):
                def so_far(i):
                    return norm_val(ln, LN_DVE, i)

                for t in range(2):
                    dve.bn_stats(stats[:, t, :], src[:, t, :]).then_inc(ln_dve, 1)
                wait_apart(dve, (ln_dve, so_far(2)))
                for t in range(2):
                    dve.bn_aggr(mv[:, t, :], stats[:, t, :]).then_inc(ln_dve, 1)
                dve.wait_ge(ln_dve, so_far(4))
                dve.tensor_scalar(var[:, :], mv[:, :, 1], EPS, None, ALU.add).then_inc(ln_dve, 1)
                dve.wait_ge(ln_dve, so_far(5))
                dve.tensor_scalar(half_var[:, :], var[:, :], -0.5, None, ALU.mult).then_inc(ln_dve, 1)
                dve.tensor_scalar(shifted[:, :], var[:, :].bitcast(I32), 1, None, ALU.logical_shift_right).then_inc(ln_dve, 1)
                dve.wait_ge(ln_dve, so_far(7))
                dve.tensor_scalar(rs[:, 0, :].bitcast(I32), shifted[:, :], -1.0, float(RSQRT_MAGIC), ALU.mult, ALU.add).then_inc(ln_dve, 1)

            def normalized(ln, src, *read):
                dve.wait_ge(ln_pool, norm_val(ln, LN_POOL, LN_POOL))
                for wait in read:
                    dve.wait_ge(*wait)
                for t in range(2):
                    dve.tensor_scalar(xn[:, t, :], src[:, t, :], mv[:, t, 0:1], rs[:, 6, t:t + 1],
                                      ALU.subtract, ALU.mult).then_inc(xn_ready, 1)

            def low(bk_tile, q, v, free):
                s_ = stg_q if q < 2 else stg_k
                g = 2 * (q % 2)
                dve.wait_ge(high_ready, v)
                dve.tensor_tensor(s_[:, :, 1, g:g + 2, :].rearrange("p t g n -> p g t n"),
                                  bk_tile[:, :].rearrange("p (g t n) -> p g t n", g=2, t=2),
                                  s_[:, :, 0, g:g + 2, :].rearrange("p t g n -> p g t n").bitcast(F32),
                                  ALU.subtract).then_inc(free, 1)

            chained(dve.memset(gt[M:M + 1, :], 1.0))
            dve.wait_ge(setup_act, 1)
            chained(dve.tensor_scalar(cs[:, 2, :], cs[:, 1, :], 1.0, None, ALU.add))
            chained(dve.reciprocal(cs[:, 1, :], cs[:, 2, :]))
            chained(dve.tensor_tensor(cs[:, 3, :], cs[:, 0, :], cs[:, 1, :], ALU.mult))
            for i in range(2):
                dve.wait_ge(setup_pe, 1 + i)
                g, a, b = gate_rows[i], rts[0:NB, :], rrep[0:NB, :, :].rearrange("p a b -> p (a b)")
                chained(dve.tensor_copy(g, d_bank[i][0:NB, :]))
                chained(dve.scalar_tensor_tensor(out=a, in0=g, scalar=-1.0, in1=g, op0=ALU.mult, op1=ALU.max))
                chained(dve.tensor_scalar(b, g, 0.0, 2.0, ALU.is_ge, ALU.mult))
                chained(dve.tensor_scalar(a, a, 0.25, None, ALU.max))
                chained(dve.scalar_tensor_tensor(out=g, in0=b, scalar=-1.0, in1=a, op0=ALU.add, op1=ALU.mult))
            assert n[0] == SETUP_GATES
            dve.wait_ge(const_done, CONST)
            for v in range(4):
                dve.wait_ge(setup_pe, 3 + v)
                src = s_bank[v % 2] if v < 2 else pt_bank[v % 2]
                chained(dve.tensor_scalar(modt[:, v, :, 1:NB + 1], src[:, 0:KD * NB].rearrange("p (k b) -> p k b", k=KD),
                                          float(v % 2), None, ALU.add))
            dve.wait_ge(w_loaded, 16 * W_LOADS)
            chained(dve.tensor_scalar(wqkv[:, :, 0:D], wqkv[:, :, 0:D], float(DH) ** -0.5, None, ALU.mult))
            for half in range(2):
                rows = slice(half * M, (half + 1) * M)
                chained(dve.tensor_copy(fold[rows, :], ident[rows, rows]))
            for i, (s_, v) in enumerate(((pt_evac[0], CREDIT_PT), (pt_evac[1], CREDIT_PT), (o_ready, CREDIT_O))):
                dve.memset(sums[:, 0, i:i + 1], 0.0).then_inc(s_, v)
            assert n[0] == SETUP_DVE

            dve.wait_ge(gates_loaded, CREDIT_G)
            dve.wait_ge(x_loaded[0], 16)
            stats_of(0, xin[:, 0, :, :])
            normalized(0, xin[:, 0, :, :])
            dve.wait_ge(x_loaded[1], 16)
            stats_of(1, xin[:, 1, :, :])
            normalized(1, xin[:, 1, :, :], (dense_ready[1], 1))
            for q in range(4):
                low(d_bank[q % 2], q, q + 1, dense_free[q % 2])

            def rowmax(s, i):
                tile, h = divmod(i, 16)
                lo = roles(s, tile)[0] * P
                if not s.first or (s.k, tile) == (1, 1):
                    m = mask
                else:
                    m = {(0, 0): mask_tile0, (0, 1): mask_tile1, (1, 0): mask_tile2}[s.k, tile]
                waits = [(s_ready, s.n(32, i + 1 + CREDIT_S))]
                if h % 4 == 0:
                    waits.append((pack_done, s.n(8, 4 * tile + h // 4 - 1 + CREDIT_PACK)))
                wait_apart(dve, *waits)
                dve.tensor_tensor_reduce(out=probs[:, h % 8, lo:LS], in0=s_bank[h % 2][:, lo:LS], in1=m[:, :],
                                         scale=-1.0, scalar=3e38, op0=ALU.add, op1=ALU.min,
                                         accum_out=negm[:, tile, h:h + 1]).then_inc(m_ready, 1)

            def evac(s, tile, h):
                lo = roles(s, tile)[0] * P
                dve.wait_ge(pt_ready[h % 2], s.n(18, 9 * tile + h // 2 + 1))
                dve.tensor_copy(pts[:, h % 8, lo:3 * P], pt_bank[h % 2][:, lo:3 * P]).then_inc(pt_evac[h % 2], 1)

            def inverse(s, tile):
                dve.wait_ge(e_ready, s.n(32, 16 * tile + 16))
                dve.reciprocal(rinv[:, :], sums[:, tile, :]).then_inc(rr_ready, 1)
                dve.wait_ge(rr_ready, s.n(4, 2 * tile + 1))
                dve.tensor_copy(rrep[:, :, :], rinv[:, :].unsqueeze(2).to_broadcast([P, HEADS, DH])).then_inc(rr_ready, 1)

            def normalize(s, tile):
                dve.wait_ge(pt_evac[1], s.n(18, 9 * tile + 9 + CREDIT_PT))
                dve.wait_ge(pv_ready, s.n(2, tile + 1 + CREDIT_PV))
                dve.tensor_tensor(ot[:, tile, :, :].rearrange("p g n -> p (g n)"), pv_bank[tile][:, :], rts[:, :],
                                  ALU.mult).then_inc(o_ready, 1)

            def gated(i, bk, which, par, free):
                dve.tensor_tensor(tmp[:, i:i + 1, :], bk[:, :].rearrange("p (a n) -> p a n", a=1),
                                  gab[:, bass.ds(par, 1), which, :], ALU.mult).then_inc(free, 1)

            def accumulate(s, j):
                dve.wait_ge(relu_ready, s.n(NJ, j + 1))
                if j == 0:
                    ins = dve.tensor_scalar(acc[:, :], relu[:, 0, :], w2c[:, 0:1], None, ALU.mult)
                else:
                    dve.wait_ge(acc_done, s.n(NJ, j))
                    ins = dve.scalar_tensor_tensor(out=acc[:, :], in0=relu[:, j % 4, :], scalar=w2c[:, j:j + 1],
                                                   in1=acc[:, :], op0=ALU.mult, op1=ALU.add)
                ins.then_inc(acc_done, 1)

            def gate_par(s):
                return dve.snap(s.o_col() % 2)

            def job(s, name):
                o_par = (s.k + 1) % 2
                if name == "LN1":
                    dve.wait_ge(x_loaded[s.k], s.base(16) + 32)
                    stats_of((s, 3), xin[:, s.k, :, :])
                elif name == "LN2":
                    dve.wait_ge(add_done, s.n(4, 2 + CREDIT_ADD))
                    stats_of((s, 2), x2[:, o_par, :, :])
                elif name == "X1":
                    normalized((s, 3), xin[:, s.k, :, :], s.ready("T2b"))
                elif name == "X2":
                    normalized((s, 2), x2[:, o_par, :, :], s.ready("T1b"))
                elif name in ("OP0", "OP1"):
                    bk = s.wait_item(name)
                    t = int(name[2])
                    if s.first and s.k == 1 and t == 0:
                        dve.wait_ge(gates_loaded, s.b * 16 + (16 + CREDIT_G))
                    dve.wait_ge(add_done, s.n(4, t - 1 + CREDIT_ADD))
                    gated(t, bk, 0, gate_par(s), dense_free[s.item(name)[0]])
                elif name in ("DN0", "DN1"):
                    bk = s.wait_item(name)
                    t = int(name[2])
                    dve.wait_ge(add_done, s.n(4, t + 1 + CREDIT_ADD))
                    gated(t, bk, 1, gate_par(s), dense_free[s.item(name)[0]])
                elif name.startswith("QK"):
                    q = int(name[2])
                    bk, _ = s.item(name)
                    low(d_bank[bk], q, s.n(4, 4 + q + 1), dense_free[bk])
                elif name == "UP":
                    bk = s.wait_item(name)
                    dve.tensor_scalar(st[:, :], bk[:, 0:CH], binc, None, ALU.add).then_inc(dense_free[s.item(name)[0]], 1)
                elif name[0] == "A":
                    accumulate(s, int(name[1]))
                elif name == "G":
                    bk = s.wait_item(name)
                    dve.tensor_scalar(gt[0:M, :], bk[0:M, 0:CH], b2c, None, ALU.add).then_inc(dense_free[s.item(name)[0]], 1)

            def step(s):
                if s.first and s.k == 0:
                    dve.wait_ge(stack_ready[0], s.base(64) + 32)
                    dve.wait_ge(s_ready, s.n(32, CREDIT_S))
                    for slot in range(4):
                        ins = dve.tensor_copy(tk[:, slot, :, :, P:P + PREFIX], tk[:, 0, :, :, 0:PREFIX].bitcast(F32))
                    ins.then_inc(prefix_keys_ready, 1)
                rowmax(s, 0)
                for i in range(32):
                    if i % 16 and (i - 1) % 16 not in ACT_EVACS:
                        evac(s, i // 16, (i - 1) % 16)
                    if i == 16:
                        inverse(s, 0)
                    if i < 31:
                        rowmax(s, i + 1)
                    if i == 17:
                        normalize(s, 0)
                    for name in DVE_SLOTS.get(i, ()):
                        job(s, name)
                inverse(s, 1)
                job(s, "DN0")
                job(s, "DN1")
                normalize(s, 1)

            run(dve, step)
            last = Step(dve, NC // 2, 0, False, NB - 1, {})

            def epi_gated(name, which):
                t = int(name[2])
                bk, v = epi_item(name)
                dve.wait_ge(dense_ready[bk], v + 1)
                dve.wait_ge(add_done, last.n(4, t - 1 + 2 * which + CREDIT_ADD))
                gated(t, d_bank[bk], which, NB % 2, dense_free[bk])

            epi_gated("OP0", 0)
            epi_gated("OP1", 0)
            dve.wait_ge(add_done, last.n(4, 2 + CREDIT_ADD))
            stats_of((last, 2), x2[:, 1, :, :])
            normalized((last, 2), x2[:, 1, :, :])
            dve.wait_ge(*epi_ready("UP"))
            bk = epi_item("UP")[0]
            dve.tensor_scalar(st[:, :], d_bank[bk][:, 0:CH], binc, None, ALU.add).then_inc(dense_free[bk], 1)
            for j in range(NJ):
                accumulate(last, j)
            dve.wait_ge(*epi_ready("G"))
            bk = epi_item("G")[0]
            dve.tensor_scalar(gt[0:M, :], d_bank[bk][0:M, 0:CH], b2c, None, ALU.add).then_inc(dense_free[bk], 1)
            epi_gated("DN0", 1)
            epi_gated("DN1", 1)

        @block.tensor
        def _(pe):
            def group(out_, pairs, start=True):
                for i, (lhsT, rhs) in enumerate(pairs):
                    ins = pe.matmul(out_, lhsT, rhs, start=start and i == 0, stop=i == len(pairs) - 1)
                return ins

            pe.wait_ge(setup_dve, SETUP_SILU)
            pe.wait_ge(m_loaded, 16 * len(mod_bufs))
            batch_cols = [cs[:, 3, k * NB:(k + 1) * NB] for k in range(KD)]
            for i, v in enumerate((2, 5)):
                group(d_bank[i][0:NB, :], [(batch_cols[k], mod_bufs[v][:, k, :]) for k in range(KD)]).then_inc(setup_pe, 1)
            for i, v in enumerate((0, 1, 3, 4)):
                bank_ = s_bank[i] if i < 2 else pt_bank[i - 2]
                for kd in range(KD):
                    ins = group(bank_[:, kd * NB:(kd + 1) * NB],
                                [(mod_bufs[v][:, k, kd * P:(kd + 1) * P], batch_cols[k]) for k in range(KD)])
                ins.then_inc(setup_pe, 1)

            def transpose_xn(bk, half):
                for i in range(2):
                    for t in range(2):
                        kd = 2 * half + i
                        ins = pe.transpose(bk[:, i * CH + t * P:i * CH + (t + 1) * P],
                                           xn[:, t, kd * P:(kd + 1) * P], ident[:, :])
                return ins

            def project_qk(bk, par, q, atom):
                gi, k = divmod(atom, KD)
                col = (q // 2) * D + (2 * (q % 2) + gi) * P
                return pe.matmul(bk[:, gi * CH:(gi + 1) * CH], wqkv[:, k, col:col + P], ht[:, par, k, :],
                                 start=k == 0, stop=k == KD - 1)

            def project_v(bk, par, t, k):
                return pe.matmul(bk[:, :], ht[:, par, k, t * P:(t + 1) * P], wqkv[:, k, 2 * D:3 * D],
                                 start=k == 0, stop=k == KD - 1)

            def out_project(bk, t, g):
                return pe.matmul(bk[:, :], ot[:, t, g, :], wo[:, g, :], start=g == 0, stop=g == G - 1)

            def ffn_up(bk, k):
                return pe.matmul(bk[:, 0:CH], win2[:, k, :], h2t[:, k, :], start=k == 0, stop=k == KD - 1)

            def ffn_hidden(s, bk):
                pe.wait_ge(acc_done, s.n(NJ, NJ))
                return pe.matmul(bk[0:M, 0:CH], fold[:, :], acc[:, :], start=True, stop=True)

            def ffn_down(bk, t):
                return pe.matmul(bk[:, :], gt[0:M + 1, t * P:(t + 1) * P], wout65[:, :], start=True, stop=True)

            pe.wait_ge(const_done, CONST)
            pe.wait_ge(w_loaded, 16 * W_LOADS)
            pe.wait_ge(setup_dve, SETUP_DVE)
            pe.wait_ge(xn_ready, 2)
            pe.transpose(d_bank[0][:, 0:P], ident[:, :], ident[:, :]).then_inc(s_ready, CREDIT_S)
            pe.transpose(d_bank[1][:, 0:P], ident[:, :], ident[:, :]).then_inc(pv_ready, CREDIT_PV)
            for half in range(2):
                transpose_xn(d_bank[half], half).then_inc(dense_ready[half], 1)
            for q in range(4):
                pe.wait_ge(dense_free[q % 2], 1 + q // 2)
                if q == 0:
                    pe.wait_ge(dense_free[1], 1)
                for atom in range(2 * KD):
                    ins = project_qk(d_bank[q % 2], 0, q, atom)
                ins.then_inc(dense_ready[q % 2], 1)
            pe.wait_ge(dense_free[0], 3)
            for k in range(KD):
                ins = project_v(d_bank[0], 0, 0, k)
            ins.then_inc(dense_ready[0], 1)

            def scores(s, i):
                tile, h = divmod(i, 16)
                j, g = h % 4, h // 4
                bk, cur = s_bank[h % 2], 2 * s.k + tile
                if h == 0:
                    pe.wait_ge(stack_ready[tile], s.n(32, 32))
                    if s.first and s.k == 0 and tile == 0:
                        pe.wait_ge(prefix_keys_ready, s.b + 1)
                queries = tq[tile][:, j, g, :]
                seen = roles(s, tile)
                runs, start = [], 0
                for n_ in range(1, len(seen)):
                    slot = (cur - 2 + seen[start]) % 4
                    if n_ == len(seen) - 1 or slot + (n_ - start) > 3:
                        runs.append((seen[start], slot, n_ - start))
                        start = n_
                for r, (block_, slot, n_) in enumerate(runs):
                    pe.matmul(bk[:, block_ * P:(block_ + n_) * P], queries, tk[:, slot:slot + n_, j, g, 0:P],
                              start=r == 0, stop=False, skip_group_check=True)
                pe.matmul(bk[:, 2 * P:LS], queries, tk[:, cur % 4, j, g, :],
                          start=not runs, stop=True, skip_group_check=True).then_inc(s_ready, 1)

            def transpose_probs(s, i):
                tile, h = divmod(i, 16)
                pe.wait_ge(e_ready, s.n(32, i + 1))
                pe.wait_ge(pt_evac[h % 2], s.n(18, 9 * tile + h // 2 + CREDIT_PT))
                for block_ in roles(s, tile):
                    ins = pe.transpose(pt_bank[h % 2][:, block_ * P:(block_ + 1) * P],
                                       probs[:, h % 8, block_ * P:(block_ + 1) * P], ident[:, :])
                ins.then_inc(pt_ready[h % 2], 1)

            def values(s, tile, g):
                for odd in range(2):
                    pe.wait_ge(pt_evac[odd], s.n(18, 9 * tile + 2 * g + 2 + CREDIT_PT))
                for n_, block_ in enumerate(roles(s, tile)):
                    slot = (2 * s.k + tile - 2 + block_) % 4
                    for j in range(4):
                        h = 4 * g + j
                        pe.matmul(pv_bank[tile][j * DH:(j + 1) * DH, g * P:(g + 1) * P],
                                  vring[:, slot, h * DH:(h + 1) * DH], pts[:, h % 8, block_ * P:(block_ + 1) * P],
                                  start=g == 0 and n_ == 0, stop=False, skip_group_check=True)

            def tail_prefix(s, tile):
                pe.wait_ge(pack_done, s.n(8, 4 * tile + 4 + CREDIT_PACK))
                pe.wait_ge(pt_evac[0], s.n(18, 9 * tile + 8 + CREDIT_PT))
                for a in range(2):
                    ins = pe.transpose(pt_bank[0][:, a * P:(a + 1) * P],
                                       ppack[:, 8 * a:8 * a + 8, :].rearrange("p h k -> p (h k)"), ident[:, :])
                ins.then_inc(pt_ready[0], 1)

            def tail_values(s, tile):
                values(s, tile, G - 1)
                pe.wait_ge(rr_ready, s.n(4, 2 * tile + 2))
                pe.wait_ge(pt_evac[1], s.n(18, 9 * tile + 8 + CREDIT_PT))
                for g in range(G):
                    ins = pe.transpose(pt_bank[1][:, g * P:(g + 1) * P],
                                       rrep[:, 4 * g:4 * g + 4, :].rearrange("p h d -> p (h d)"), ident[:, :])
                ins.then_inc(pt_ready[1], 1)
                if s.first and s.k == 0 and tile == 0:
                    pe.wait_ge(vp_loaded, s.b * (16 * HEADS) + 16 * HEADS)
                pe.wait_ge(pt_evac[0], s.n(18, 9 * tile + 9 + CREDIT_PT))
                for g in range(G):
                    ins = pe.matmul(pv_bank[tile][:, g * P:(g + 1) * P], vp[:, g, :], ptp[:, g // 2, :],
                                    start=False, stop=True, skip_group_check=True)
                ins.then_inc(pv_ready, 1)

            def dense(s, name, atom):
                bk, v = s.item(name)
                bank_ = d_bank[bk]
                if atom == 0:
                    pe.wait_ge(dense_free[bk], v)
                    if name == "QK0":
                        s.wait_taken("T1a")
                    elif name == "UP":
                        s.wait_taken("T2b")
                    elif name in ("OP0", "OP1"):
                        pe.wait_ge(o_ready, s.n(2, int(name[2]) - 1 + CREDIT_O))
                    elif name[0] == "T":
                        pe.wait_ge(xn_ready, s.n(4, 2 + 2 * int(name[1])))
                    elif name == "DN0":
                        s.wait_taken("G")
                if name in ("T1a", "T2a", "T1b", "T2b"):
                    ins = transpose_xn(bank_, "ab".index(name[2]))
                elif name.startswith("QK"):
                    ins = project_qk(bank_, (s.k + 1) % 2, int(name[2]), atom)
                elif name == "V1":
                    ins = project_v(bank_, s.k, 1, atom)
                elif name == "V2":
                    ins = project_v(bank_, (s.k + 1) % 2, 0, atom)
                elif name in ("OP0", "OP1"):
                    ins = out_project(bank_, int(name[2]), atom)
                elif name == "UP":
                    ins = ffn_up(bank_, atom)
                elif name == "G":
                    ins = ffn_hidden(s, bank_)
                else:
                    ins = ffn_down(bank_, int(name[2]))
                if atom == ATOMS[name] - 1:
                    ins.then_inc(dense_ready[bk], 1)

            def step(s):
                scores(s, 0)
                for i in range(32):
                    if i < 31:
                        scores(s, i + 1)
                    for name, part in PE_SLOTS.get(i, ()):
                        dense(s, name, part)
                    if i == 16:
                        tail_values(s, 0)
                    transpose_probs(s, i)
                    if i % 4 == 1 and i % 16 > 4:
                        values(s, i // 16, i % 16 // 4 - 1)
                    if i == 15:
                        tail_prefix(s, 0)
                tail_prefix(s, 1)
                dense(s, "DN1", 0)
                tail_values(s, 1)

            run(pe, step)
            last = Step(pe, NC // 2, 0, False, NB - 1, {})
            for name in EPI:
                bk, v = epi_item(name)
                bank_ = d_bank[bk]
                pe.wait_ge(dense_free[bk], v)
                if name in ("OP0", "OP1"):
                    pe.wait_ge(o_ready, last.n(2, int(name[2]) - 1 + CREDIT_O))
                elif name in ("T2a", "T2b"):
                    pe.wait_ge(xn_ready, last.n(4, 6))
                elif name == "UP":
                    pe.wait_ge(*epi_taken("T2b"))
                elif name == "DN0":
                    pe.wait_ge(*epi_taken("G"))
                for atom in range(ATOMS[name]):
                    if name in ("OP0", "OP1"):
                        ins = out_project(bank_, int(name[2]), atom)
                    elif name in ("T2a", "T2b"):
                        ins = transpose_xn(bank_, "ab".index(name[2]))
                    elif name == "UP":
                        ins = ffn_up(bank_, atom)
                    elif name == "G":
                        ins = ffn_hidden(last, bank_)
                    else:
                        ins = ffn_down(bank_, int(name[2]))
                ins.then_inc(dense_ready[bk], 1)


def kernel(L0_attn_x, L0_attn_w_qkv, L0_attn_w_out, L0_ffn_Win, L0_ffn_bin_, L0_ffn_W1, L0_ffn_b1, L0_ffn_W2,
           L0_ffn_b2, L0_ffn_Wout, L0_ffn_bout, L0_c, L0_wmod):
    import numpy as np
    import concourse.bacc as bacc
    from concourse.bass_utils import run_bass_kernel_spmd

    arrays = {
        "x": np.ascontiguousarray(L0_attn_x),
        "w_qkv_t": np.ascontiguousarray(np.asarray(L0_attn_w_qkv).T),
        "w_out_t": np.ascontiguousarray(np.asarray(L0_attn_w_out).T),
        "win": np.ascontiguousarray(L0_ffn_Win),
        "bin": np.ascontiguousarray(L0_ffn_bin_),
        "w1": np.ascontiguousarray(L0_ffn_W1),
        "b1": np.ascontiguousarray(L0_ffn_b1),
        "w2": np.ascontiguousarray(L0_ffn_W2),
        "b2": np.ascontiguousarray(L0_ffn_b2),
        "wout": np.ascontiguousarray(L0_ffn_Wout),
        "bout": np.ascontiguousarray(L0_ffn_bout),
        "c_t": np.ascontiguousarray(np.asarray(L0_c).T),
        "wmod": np.ascontiguousarray(L0_wmod),
    }
    nc = bacc.Bacc("TRN2", target_bir_lowering=False, num_devices=1)
    args = [nc.dram_tensor("in_" + name, array.shape, F32, kind="ExternalInput").ap() for name, array in arrays.items()]
    out = nc.dram_tensor("out_0", arrays["x"].shape, F32, kind="ExternalOutput").ap()
    attention_block(nc, *args, out)
    result = run_bass_kernel_spmd(nc, [{"in_" + name: array for name, array in arrays.items()}], core_ids=[0])
    return result.results[0]["out_0"]
```
